# Optimizing a Trainium2 kernel written in Bass

```python
import numpy as np
import jax
import jax.numpy as jnp

def _softmax(x, axis=-1):
    return jax.nn.softmax(x, axis=axis)

def _gelu(x):
    return jax.nn.gelu(x, approximate=True)

def _silu(x):
    return jax.nn.silu(x)

def _sigmoid(x):
    return jax.nn.sigmoid(x)

def _layernorm(x, axis=-1, eps=1e-05):
    m = jnp.mean(x, axis=axis, keepdims=True)
    v = jnp.var(x, axis=axis, keepdims=True)
    return (x - m) / jnp.sqrt(v + eps)

def _scatter_add(tgt, idx, src, axis=0):
    return tgt.at[idx].add(src)

def _segment_sum(src, seg, n):
    return jax.ops.segment_sum(src, seg, n)
kernel_name = 'mk_xattn_ffn_d1_seqx_r2_6bf6b0'

def setup_inputs(seed: int=0):
    np.random.seed(seed)
    _w = jnp.asarray

    def _rec_inputs():
        import jax
        import jax.numpy as jnp
        _rk = jax.random.key(seed)
        x = -0.000125 + 0.9999 * jax.random.normal(jax.random.fold_in(_rk, 1), (32, 512, 512), jnp.float32)
        _lenS = 512 - jax.random.randint(jax.random.fold_in(_rk, 7), (32,), 0, max(1, 512 // 4) + 1, jnp.int32)
        _lenS2 = 512 - jax.random.randint(jax.random.fold_in(_rk, 8), (32,), 0, max(1, 512 // 4) + 1, jnp.int32)
        _ctx_1024P = jax.random.normal(jax.random.fold_in(_rk, 11), (32, 16, 512), jnp.float32)
        _ctx_1024c = jax.random.dirichlet(jax.random.fold_in(_rk, 511), 0.3 * jnp.ones((16,), jnp.float32), (32, 512))
        _ctx_1024t = jnp.einsum('bsk,bkd->bsd', _ctx_1024c, _ctx_1024P)
        _ctx_1024t = _ctx_1024t * jax.lax.rsqrt(jnp.mean(jnp.square(_ctx_1024t)) + 1e-12) * 0.953939
        ctx_1024 = -1.52775e-05 + 0.999936 * (_ctx_1024t + 0.3 * jax.random.normal(jax.random.fold_in(_rk, 611), (32, 512, 512), jnp.float32))
        return (x, ctx_1024)
    x, ctx_1024 = _rec_inputs()

    def _L0_xattn_setup():
        import jax, jax.numpy as jnp
        import numpy as np
        DECAY = 0.9
        key = jax.random.key(seed)
        k1, k2, k3 = jax.random.split(key, 3)
        B, S, D = (8, 2048, 512)
        q = jax.random.normal(k1, (B, S, D), dtype=jnp.float32)
        k = jax.random.normal(k2, (B, S, D), dtype=jnp.float32)
        v = jax.random.normal(k3, (B, S, D), dtype=jnp.float32)
        return {'q': q, 'k': k, 'v': v}
    _L0_xattn_all = _L0_xattn_setup()
    _L0_xattn_in = {k: v for k, v in _L0_xattn_all.items() if k in ()}
    del _L0_xattn_all

    def _L0_ffn_setup():
        import jax, jax.numpy as jnp
        import numpy as np
        D_MODEL = 512
        EXPANSION = 4
        D_HIDDEN = D_MODEL * EXPANSION
        NUM_STAGES = int(np.log2(D_HIDDEN))

        def butterfly(y, weights, dim):
            lead = y.shape[:-1]
            for stage in range(weights.shape[0]):
                s = 2 ** stage
                nb = dim // (2 * s)
                yr = y.reshape(*lead, nb, 2, s)
                a = yr[..., 0, :]
                b = yr[..., 1, :]
                w = weights[stage].reshape(nb, s, 2, 2)
                na = w[..., 0, 0] * a + w[..., 0, 1] * b
                nb2 = w[..., 1, 0] * a + w[..., 1, 1] * b
                y = jnp.stack([na, nb2], axis=-2).reshape(*lead, dim)
            return y
        key = jax.random.key(seed)
        ks = jax.random.split(key, 6)
        B, S = (4, 1024)
        x = jax.random.normal(ks[0], (B, S, D_MODEL), jnp.float32)
        W_exp = jax.random.normal(ks[1], (D_MODEL, D_HIDDEN), jnp.float32) * 0.02
        b_exp = jnp.zeros((D_HIDDEN,), jnp.float32)
        up_weights = jax.random.normal(ks[2], (NUM_STAGES, D_HIDDEN // 2, 2, 2), jnp.float32) * 0.02
        up_bias = jnp.zeros((D_HIDDEN,), jnp.float32)
        down_weights = jax.random.normal(ks[3], (NUM_STAGES, D_HIDDEN // 2, 2, 2), jnp.float32) * 0.02
        W_con = jax.random.normal(ks[4], (D_HIDDEN, D_MODEL), jnp.float32) * 0.02
        b_con = jnp.zeros((D_MODEL,), jnp.float32)
        down_bias = jnp.zeros((D_MODEL,), jnp.float32)
        return dict(x=x, W_exp=W_exp, b_exp=b_exp, up_weights=up_weights, up_bias=up_bias, down_weights=down_weights, W_con=W_con, b_con=b_con, down_bias=down_bias)
    _L0_ffn_all = _L0_ffn_setup()
    _L0_ffn_in = {k: v for k, v in _L0_ffn_all.items() if k in ('W_exp', 'b_exp', 'up_weights', 'up_bias', 'down_weights', 'W_con', 'b_con', 'down_bias')}
    del _L0_ffn_all
    return {'x': x, 'ctx_1024': ctx_1024, 'L0_ffn_W_exp': _L0_ffn_in['W_exp'], 'L0_ffn_b_exp': _L0_ffn_in['b_exp'], 'L0_ffn_up_weights': _L0_ffn_in['up_weights'], 'L0_ffn_up_bias': _L0_ffn_in['up_bias'], 'L0_ffn_down_weights': _L0_ffn_in['down_weights'], 'L0_ffn_W_con': _L0_ffn_in['W_con'], 'L0_ffn_b_con': _L0_ffn_in['b_con'], 'L0_ffn_down_bias': _L0_ffn_in['down_bias']}

def reference(x, ctx_1024, L0_ffn_W_exp, L0_ffn_b_exp, L0_ffn_up_weights, L0_ffn_up_bias, L0_ffn_down_weights, L0_ffn_W_con, L0_ffn_b_con, L0_ffn_down_bias):
    import jax
    import jax.numpy as jnp

    def _L0_xattn_ref(q, k, v):
        import jax, jax.numpy as jnp
        import numpy as np
        DECAY = 0.9
        kv = jnp.swapaxes(k * v, 0, 1)

        def step(r, kv_t):
            r = DECAY * r + kv_t
            return (r, r)
        r0 = jnp.zeros(q.shape[:1] + q.shape[2:], dtype=q.dtype)
        _, rs = jax.lax.scan(step, r0, kv)
        return q * jnp.swapaxes(rs, 0, 1)

    def _L0_ffn_ref(x, W_exp, b_exp, up_weights, up_bias, down_weights, W_con, b_con, down_bias):
        import jax, jax.numpy as jnp
        import numpy as np
        D_MODEL = 512
        EXPANSION = 4
        D_HIDDEN = D_MODEL * EXPANSION
        NUM_STAGES = int(np.log2(D_HIDDEN))

        def butterfly(y, weights, dim):
            lead = y.shape[:-1]
            for stage in range(weights.shape[0]):
                s = 2 ** stage
                nb = dim // (2 * s)
                yr = y.reshape(*lead, nb, 2, s)
                a = yr[..., 0, :]
                b = yr[..., 1, :]
                w = weights[stage].reshape(nb, s, 2, 2)
                na = w[..., 0, 0] * a + w[..., 0, 1] * b
                nb2 = w[..., 1, 0] * a + w[..., 1, 1] * b
                y = jnp.stack([na, nb2], axis=-2).reshape(*lead, dim)
            return y
        h = jnp.einsum('bsd,dh->bsh', x, W_exp) + b_exp
        h = butterfly(h, up_weights, D_HIDDEN)
        h = jax.nn.gelu(h + up_bias, approximate=False)
        h = butterfly(h, down_weights, D_HIDDEN)
        y = jnp.einsum('bsh,hd->bsd', h, W_con) + b_con
        return y + down_bias
    x = x + _L0_xattn_ref(_layernorm(x, axis=-1), ctx_1024, ctx_1024)
    x = x + _L0_ffn_ref(_layernorm(x, axis=-1), L0_ffn_W_exp, L0_ffn_b_exp, L0_ffn_up_weights, L0_ffn_up_bias, L0_ffn_down_weights, L0_ffn_W_con, L0_ffn_b_con, L0_ffn_down_bias)
    return x

_drawn_inputs = setup_inputs


def setup_inputs(seed=0):
    import zlib

    import numpy as np

    out = dict(_drawn_inputs(seed))
    spreads = {'L0_ffn_b_exp': (0.0, 0.1),
     'L0_ffn_up_bias': (0.0, 0.1),
     'L0_ffn_b_con': (0.0, 0.8),
     'L0_ffn_down_bias': (0.0, 0.8)}
    factors = {}
    for name, (base, spread) in spreads.items():
        noise = np.random.default_rng([zlib.crc32(name.encode()), seed]).standard_normal(out[name].shape)
        drawn = base * np.exp(spread * noise) if base else spread * noise
        out[name] = jnp.asarray(drawn.astype(out[name].dtype))
    for name, factor in factors.items():
        out[name] = (out[name] * factor).astype(out[name].dtype)
    return out
```

```python
import concourse.bass as bass
from concourse import mybir
from contextlib import ExitStack


def xattn_ffn_program(nc, x_in, ctx_in, w_exp, b_exp, up_w, up_bias, down_w, w_con, b_con, down_bias, out):
    f32 = mybir.dt.float32
    f32r = mybir.dt.float32r
    i32 = mybir.dt.int32
    ALU = mybir.AluOpType
    ACT = mybir.ActivationFunctionType

    P = 128
    B, S, D = x_in.shape
    H = w_exp.shape[1]
    KD = D // P
    KH = H // P
    LOW = 7
    HIGH = up_w.shape[0] - LOW
    PAIRS = KH // 2
    G = 4
    Q = 32
    J = 4
    T = B * S // (J * P)
    STEPS_PER_BATCH = S // (Q * J)
    DECAY = 0.9
    EPS = 1e-5
    LAG = 2
    NX = 16

    def token_rows(a):
        return a.rearrange("b s d -> (b s) d").rearrange("(g t j i) d -> g t i j d", g=G, t=T, j=J, i=Q)

    x_rows, ctx_rows, out_rows = token_rows(x_in), token_rows(ctx_in), token_rows(out)

    es = ExitStack()
    with es:
        def sb(name, shape, dt=f32, stack=es):
            return stack.enter_context(nc.sbuf_tensor(name, shape, dt))

        def sem(name):
            return es.enter_context(nc.semaphore(name))

        fold = ExitStack()
        wexp = sb("wexp", [P, KD, H], stack=fold)
        lowsrc_dn = sb("lowsrc_dn", [P, 4 * H], stack=fold)
        wcon = sb("wcon", [P, KH, D], stack=fold)
        Y = sb("Y", [P, KH, D], stack=fold)
        lowsrc_up = Y[:, :, :].rearrange("p k d -> p (k d)")
        X_up = sb("X_up", [P, KH, P], stack=fold)
        X_dn = sb("X_dn", [P, KH, P], stack=fold)
        tmp = sb("tmp", [P, 8, D], stack=fold)
        X_half = sb("X_half", [P, KH * P // 2], stack=fold)
        sel = sb("sel", [P, LOW, 2, P], stack=fold)
        fold.close()
        W1hi = sb("W1hi", [P, KH, KD, P], f32r)
        W1lo = sb("W1lo", [P, KH, KD, P], f32r)
        W2hi = sb("W2hi", [P, KH, D], f32r)
        W2lo = sb("W2lo", [P, KH, D], f32r)
        xThi, xTlo = [], []
        for par in range(2):
            xThi.append(sb(f"xThi{par}", [P, KD, J * P], f32r))
            xTlo.append(sb(f"xTlo{par}", [P, KD, J * P], f32r))
        g32 = sb("g32", [P, 2, J * P])
        ghi = sb("ghi", [P, 2, J * P], f32r)
        glo = sb("glo", [P, 2, J * P], f32r)
        xs = [sb(f"x{par}", [P, J, D]) for par in range(2)]
        kv = sb("kv", [P, J, D])
        kvT = sb("kvT", [P, D // Q, Q])
        decay = sb("decay", [P, D])
        bias_row = sb("bias_row", [P, D])
        ident = sb("ident", [P, P])
        carry = sb("carry", [P, D // Q])
        keep = sb("keep", [P, T + 1], i32)
        st1 = sb("st1", [P, J, 6])
        mv1 = sb("mv1", [P, J, 2])
        ve1 = sb("ve1", [P, J])
        rstd1 = sb("rstd1", [P, J])
        st2 = sb("st2", [P, J, 6])
        mv2 = sb("mv2", [P, J, 2])
        ve2 = sb("ve2", [P, J])
        rstd2 = sb("rstd2", [P, J])
        neg_half = sb("neg_half", [P, J])
        wait_pad = sb("wait_pad", [P, J + 1])
        eps = sb("eps", [P, J])
        gelu_bias = sb("gelu_bias", [P, KH])
        flat1 = xs[1][:, :, :].rearrange("p j d -> p (j d)")
        hc_up = flat1[:, 0:HIGH * PAIRS * 4].rearrange("p (s m e) -> p s m e", s=HIGH, m=PAIRS)
        hc_dn = flat1[:, 128:128 + HIGH * PAIRS * 4].rearrange("p (s m e) -> p s m e", s=HIGH, m=PAIRS)
        bias_rows = flat1[0:2 * KH, 256:256 + P]
        bcol = flat1[:, 384:384 + 2 * KH]
        yb = flat1[:, 448:448 + KH]
        ybt = flat1[:, 512:512 + 4 * PAIRS].rearrange("p (e m) -> p e m", e=4)
        bias_tmp = flat1[:, 1024:1024 + D]

        ps = [es.enter_context(nc.psum_tensor(f"ps{i}", [P, 512], f32)) for i in range(8)]
        ps_h, ps_t, ps_y = ps[0:2], ps[2:4], ps[4:8]

        low_loaded = [sem("low_up_loaded"), sem("low_dn_loaded")]
        coef_loaded = sem("coef_loaded")
        bias_loaded = sem("bias_loaded")
        wexp_loaded = sem("wexp_loaded")
        wcon_loaded = sem("wcon_loaded")
        x_loaded = sem("x_loaded")
        ctx_loaded = sem("ctx_loaded")
        out_stored = sem("out_stored")
        ident_zero = sem("ident_zero")
        ident_ready = sem("ident_ready")
        sel_zero = sem("sel_zero")
        sel_ready = sem("sel_ready")
        const_ready = sem("const_ready")
        const_base = sem("const_base")
        neg_ready = sem("neg_ready")
        coef_spread = sem("coef_spread")
        low_product = sem("low_product")
        dn_turned = sem("dn_turned")
        dn_kept = sem("dn_kept")
        bcol_turned = sem("bcol_turned")
        bcol_kept = sem("bcol_kept")
        bias_low = sem("bias_low")
        yb_kept = sem("yb_kept")
        yb_step = sem("yb_step")
        gelu_bias_ready = sem("gelu_bias_ready")
        wt_turned = sem("wt_turned")
        wt_kept = [sem("wt_kept_act"), sem("wt_kept_dve")]
        low_mixed = sem("low_mixed")
        low_kept = [sem("low_kept_act"), sem("low_kept_dve")]
        scaled = [sem("scaled_up"), sem("scaled_dn")]
        mixed = [sem("mixed_up"), sem("mixed_dn")]
        w1_turned = sem("w1_turned")
        w1hi_ready = sem("w1hi_ready")
        w1lo_ready = sem("w1lo_ready")
        w2_mixed = sem("w2_mixed")
        w2hi_ready = sem("w2hi_ready")
        w2lo_ready = sem("w2lo_ready")
        bias_row_ready = sem("bias_row_ready")

        squared = sem("squared")
        kv_turned = sem("kv_turned")
        carry_added = sem("carry_added")
        scanned = sem("scanned")
        carry_saved = sem("carry_saved")
        gate_turned = sem("gate_turned")
        stats1_done = sem("stats1_done")
        mean1_ready = sem("mean1_ready")
        eps1_added = sem("eps1_added")
        rstd1_ready = sem("rstd1_ready")
        gated = sem("gated")
        x1_ready = sem("x1_ready")
        stats2_done = sem("stats2_done")
        mean2_ready = sem("mean2_ready")
        eps2_added = sem("eps2_added")
        rstd2_ready = sem("rstd2_ready")
        xn_ready = sem("xn_ready")
        bias_added = sem("bias_added")
        xT_turned = sem("xT_turned")
        xThi_ready = sem("xThi_ready")
        xTlo_ready = sem("xTlo_ready")
        h_ready = sem("h_ready")
        gelu_ready = sem("gelu_ready")
        ghi_ready = sem("ghi_ready")
        glo_ready = sem("glo_ready")
        y_part = sem("y_part")
        out_ready = sem("out_ready")

        def wait(eng, semaphore, value):
            if isinstance(value, int) and value <= 0:
                return
            eng.wait_ge(semaphore, value)

        block = es.enter_context(nc.Block())

        def steps(eng, body):
            body(0, 0, first=True, last=False)
            with eng.Fori(1, T - 1, 2) as t:
                body(t, 1, first=False, last=False)
                body(t + 1, 0, first=False, last=False)
            body(T - 1, (T - 1) % 2, first=False, last=True)

        def high_plan(order):
            written, plan, n = {}, [], 0
            for bit in order:
                for m in range(PAIRS):
                    a = ((m >> bit) << (bit + 1)) | (m & ((1 << bit) - 1))
                    b = a | (1 << bit)
                    plan.append((bit, m, a, b, written.get(a, 0), written.get(b, 0)))
                    n += 2
                    written[a], written[b] = n - 1, n
            return plan, written

        up_plan, up_written = high_plan(range(HIGH))
        dn_plan, dn_written = high_plan(reversed(range(HIGH)))
        W1_ORDER = sorted(range(KH), key=lambda k: up_written[k])
        W2_ORDER = sorted(range(KH), key=lambda k: dn_written[k])

        def low_src(stage):
            n = 4 * KH << stage
            return (P // 2) >> stage, n - 4 * KH, n

        def spread_place(stage):
            return {0: (1, 448), 1: (1, 384), 2: (1, 256), 3: (1, 0), 4: (0, 0), 5: (2, 0), 6: (4, 0)}[stage]

        @block.sync
        def _(sp):
            def load_low(weights, dst, loaded):
                for stage in range(LOW):
                    rows, off, n = low_src(stage)
                    src = weights[stage].rearrange("(k q l) a b -> q k (l a b)", k=KH, q=rows)
                    sp.dma_start(dst[0:rows, off:off + n].rearrange("q (k n) -> q k n", k=KH), src)\
                      .then_inc(loaded, NX)

            def load_tokens(dst, rows, t, loaded):
                for g in range(G):
                    sp.dma_start(dst[Q * g:Q * g + Q, :, :], rows[g, t]).then_inc(loaded, NX)

            load_low(up_w, lowsrc_up, low_loaded[0])
            for c in range(KD):
                sp.dma_start(wexp[:, c, :], w_exp[c * P:(c + 1) * P, :]).then_inc(wexp_loaded, NX)
            load_low(down_w, lowsrc_dn, low_loaded[1])
            wcon_src = w_con.rearrange("(k p) d -> p k d", p=P)
            for c in range(0, KH, 4):
                sp.dma_start(wcon[:, c:c + 4, :], wcon_src[:, c:c + 4, :]).then_inc(wcon_loaded, NX)
            load_tokens(kv, ctx_rows, 0, ctx_loaded)
            load_tokens(xs[0], x_rows, 0, x_loaded)
            sp.wait_ge(xT_turned, J)
            load_tokens(kv, ctx_rows, 1, ctx_loaded)

            def body(t, par, first, last):
                if first:
                    sp.wait_ge(w2lo_ready, KH)
                    sp.wait_ge(gelu_bias_ready, 1)
                else:
                    sp.wait_ge(out_ready, t * J)
                    for g in range(G):
                        sp.dma_start(out_rows[g, t - 1], xs[1 - par][Q * g:Q * g + Q, :, :])\
                          .then_inc(out_stored, NX)
                if not last:
                    if not first:
                        sp.wait_ge(out_stored, t * (G * NX))
                    load_tokens(xs[1 - par], x_rows, t + 1, x_loaded)

            def next_ctx(t):
                sp.wait_ge(xT_turned, (t + 2) * J)
                load_tokens(kv, ctx_rows, t + 2, ctx_loaded)

            body(0, 0, True, False)
            next_ctx(0)
            with sp.Fori(1, T - 3, 2) as t:
                body(t, 1, False, False)
                next_ctx(t)
                body(t + 1, 0, False, False)
                next_ctx(t + 1)
            body(T - 3, (T - 3) % 2, False, False)
            next_ctx(T - 3)
            body(T - 2, (T - 2) % 2, False, False)
            body(T - 1, (T - 1) % 2, False, True)
            sp.wait_ge(out_ready, T * J)
            for g in range(G):
                sp.dma_start(out_rows[g, T - 1], xs[(T - 1) % 2][Q * g:Q * g + Q, :, :]).then_inc(out_stored, NX)
            sp.wait_ge(out_stored, T * G * NX)

        @block.gpsimd
        def _(pool):
            nc.gpsimd.memset(ident[:, :], 0.0).then_inc(ident_zero, 1)
            nc.gpsimd.memset(sel[:, :, :, :], 0.0).then_inc(sel_zero, 1)
            pool.wait_ge(ident_zero, 1)
            nc.gpsimd.affine_select(out=ident[:, :], in_=ident[:, :], compare_op=ALU.not_equal, fill=1.0, base=0,
                                    pattern=[[-1, P]], channel_multiplier=1).then_inc(ident_ready, 1)
            pool.wait_ge(sel_zero, 1)
            for stage in range(LOW):
                rows = (P // 2) >> stage
                for bit in range(2):
                    v = sel[0:rows, stage, bit, :].rearrange("q (a b) -> q a b", b=1 << stage)
                    nc.gpsimd.affine_select(out=v, in_=v, compare_op=ALU.not_equal, fill=1.0, base=bit,
                                            pattern=[[-1, P >> stage], [0, 1 << stage]], channel_multiplier=2)\
                        .then_inc(sel_ready, 1)
            nc.gpsimd.memset(neg_half[:, :], -0.5).then_inc(neg_ready, 1)
            nc.gpsimd.memset(eps[:, :], EPS).then_inc(neg_ready, 1)

            pool.wait_ge(coef_loaded, 2 * NX)
            pool.wait_ge(yb_kept, 1)
            n = 0

            def step(ins):
                nonlocal n
                n += 1
                ins.then_inc(yb_step, 1)

            for bit in range(HIGH):
                v = yb.rearrange("p (h s l) -> p h s l", s=2, l=1 << bit)
                c = hc_up[:, bit, :, :].rearrange("p (h l) e -> p h l e", l=1 << bit)
                tt = ybt.rearrange("p e (h l) -> p e h l", l=1 << bit)
                if n:
                    pool.wait_ge(yb_step, n)
                for e in range(4):
                    step(nc.gpsimd.tensor_tensor(out=tt[:, e], in0=v[:, :, e % 2, :], in1=c[:, :, :, e], op=ALU.mult))
                pool.wait_ge(yb_step, n)
                for o in range(2):
                    step(nc.gpsimd.tensor_tensor(out=v[:, :, o, :], in0=tt[:, 2 * o], in1=tt[:, 2 * o + 1], op=ALU.add))
            pool.wait_ge(yb_step, n)
            nc.gpsimd.tensor_tensor(out=gelu_bias[:, :], in0=yb, in1=bcol[:, KH:2 * KH], op=ALU.add)\
                .then_inc(gelu_bias_ready, 1)

            def rstd(u):
                pool.wait_ge(mean1_ready, u * J + J)
                nc.gpsimd.tensor_tensor(out=ve1[:, :], in0=mv1[:, :, 1], in1=eps[:, :], op=ALU.add).then_inc(eps1_added, 1)
                pool.wait_ge(eps1_added, u + 1)
                nc.gpsimd.tensor_tensor(out=rstd1[:, :], in0=ve1[:, :], in1=neg_half[:, :], op=ALU.pow)\
                    .then_inc(rstd1_ready, 1)
                for j in range(J):
                    pool.wait_ge(mean2_ready, u * J + j + 1)
                    nc.gpsimd.tensor_tensor(out=ve2[:, j:j + 1], in0=mv2[:, j, 1:2], in1=eps[:, j:j + 1], op=ALU.add)\
                        .then_inc(eps2_added, 1)
                    pool.wait_ge(eps2_added, u * J + j + 1)
                    nc.gpsimd.tensor_tensor(out=rstd2[:, j:j + 1], in0=ve2[:, j:j + 1], in1=neg_half[:, j:j + 1],
                                            op=ALU.pow).then_inc(rstd2_ready, 1)

            pool.wait_ge(neg_ready, 2)
            rstd(0)
            with pool.Fori(1, T) as u:
                rstd(u)

        @block.scalar
        def _(act):
            def high_coefs(dst, weights):
                src = weights[LOW:LOW + HIGH].rearrange("s (m p) a b -> p s m (a b)", p=P)
                act.dma_start(dst, src).then_inc(coef_loaded, NX)

            high_coefs(hc_up, up_w)
            high_coefs(hc_dn, down_w)
            act.dma_start(bias_rows[0:KH, :], b_exp.rearrange("(k p) -> k p", p=P)).then_inc(bias_loaded, NX)
            act.dma_start(bias_rows[KH:2 * KH, :], up_bias.rearrange("(k p) -> k p", p=P)).then_inc(bias_loaded, NX)
            act.dma_start(bias_row[:, :], b_con.partition_broadcast(P)).then_inc(bias_loaded, NX)
            act.dma_start(bias_tmp, down_bias.partition_broadcast(P)).then_inc(bias_loaded, NX)

            act.wait_ge(bcol_turned, 1)
            act.activation(bcol, ps[6][:, 0:2 * KH], ACT.Copy).then_inc(bcol_kept, 1)
            for q in range(KH // 4):
                act.wait_ge(dn_turned, q + 1)
                act.activation(X_dn[:, 4 * q:4 * q + 4, :], ps[q][:, :].rearrange("p (k h) -> p k h", k=4), ACT.Copy)\
                   .then_inc(dn_kept, 1)
            for i in range(KH + 2):
                if i < KH and i % 2 == 0:
                    act.wait_ge(wt_turned, i + 1)
                    act.activation(Y[:, i, :], ps[4][:, :], ACT.Copy).then_inc(wt_kept[0], 1)
                k = i - 2
                if k >= 0 and k % 2 == 0:
                    act.wait_ge(low_mixed, k + 1)
                    act.activation(Y[:, k, :], ps[k % 4][:, :], ACT.Copy).then_inc(low_kept[0], 1)
            act.wait_ge(bias_low, 1)
            act.activation(yb, ps[7][:, 0:KH], ACT.Copy).then_inc(yb_kept, 1)

            def high_products(plan, buf, coef, dn):
                act.wait_ge(coef_loaded, 2 * NX)
                for q, (bit, m, a, b, wa, wb) in enumerate(plan):
                    wait(act, mixed[dn], max(wa, 2 * q - 6))
                    if not dn and bit == 0:
                        act.wait_ge(low_kept[0], a // 2 + 1)
                    for o in range(2):
                        e = o if dn else 2 * o
                        act.activation(tmp[:, (2 * q + o) % 8, :], buf[:, a, :], ACT.Copy,
                                       scale=coef[:, bit, m, e:e + 1]).then_inc(scaled[dn], 1)

            high_products(up_plan, Y, hc_up, 0)
            for i, k in enumerate(W1_ORDER):
                act.wait_ge(w1_turned, i + 1)
                act.activation(W1hi[:, k, :, :], ps[i % 4][:, :].rearrange("p (c h) -> p c h", c=KD), ACT.Copy)\
                   .then_inc(w1hi_ready, 1)
            act.wait_ge(wcon_loaded, KH // 4 * NX)
            act.wait_ge(mixed[0], len(up_plan) * 2)
            high_products(dn_plan, wcon, hc_dn, 1)
            for i, k in enumerate(W2_ORDER):
                act.wait_ge(w2_mixed, i + 1)
                act.activation(W2hi[:, k, :], ps[4 + i % 4][:, :], ACT.Copy).then_inc(w2hi_ready, 1)

            def square(u):
                act.wait_ge(ctx_loaded, (u + 1) * (G * NX))
                act.activation(kv[:, :, :], kv[:, :, :], ACT.Square).then_inc(squared, 1)

            def keep_xT_hi(u, par, j):
                act.wait_ge(xT_turned, u * J + j + 1)
                act.activation(xThi[par][:, :, j * P:(j + 1) * P],
                               ps_t[j % 2][:, :].rearrange("p (c n) -> p c n", c=KD), ACT.Copy)\
                   .then_inc(xThi_ready, 1)

            square(0)
            for j in range(J):
                keep_xT_hi(0, 0, j)
            act.wait_ge(gelu_bias_ready, 1)

            def body(t, par, first, last):
                for k in range(KH):
                    if k == 0 and not last:
                        square(t + 1)
                    s = t * KH + k
                    act.wait_ge(h_ready, s + 1)
                    wait(act, glo_ready, s - 1)
                    act.activation(g32[:, k % 2, :], ps_h[k % 2][:, :], ACT.Gelu, bias=gelu_bias[:, k:k + 1])\
                       .then_inc(gelu_ready, 1)
                    if not last and 10 <= k < 10 + J:
                        keep_xT_hi(t + 1, 1 - par, k - 10)

            steps(act, body)

        @block.vector
        def _(dve):
            nc.vector.memset(decay[:, :], DECAY).then_inc(const_base, 1)
            nc.vector.memset(keep[:, :], -1).then_inc(const_base, 1)
            nc.vector.memset(carry[:, :], 0.0).then_inc(carry_saved, 1)
            dve.wait_ge(const_base, 2)
            nc.vector.memset(decay[:, :].rearrange("p (b i) -> p b i", i=Q)[:, :, 0:1], 0.0).then_inc(const_ready, 1)
            nc.vector.memset(keep[:, STEPS_PER_BATCH - 1:T:STEPS_PER_BATCH], 0).then_inc(const_ready, 1)

            def low_matrix(X, dn):
                prev = None
                for stage in range(LOW):
                    n = KH << (stage + 1)
                    cur = (X[:, :, :].rearrange("p k j -> p (k j)") if (LOW - 1 - stage) % 2 == 0 else X_half[:, :])[:, 0:n]
                    bank, col = spread_place(stage)
                    count = dn * LOW + stage
                    dve.wait_ge(coef_spread, dn * LOW + max(stage, 3) + 1)
                    if prev is None:
                        nc.vector.tensor_copy(cur, ps[bank][:, col:col + n]).then_inc(low_product, 1)
                    else:
                        dve.wait_ge(low_product, count)
                        kb = max(1, n // 512)
                        kn = KH // kb
                        for c in range(kb):
                            o = cur.rearrange("p (k a l) -> p k a l", k=KH, a=2)[:, c * kn:(c + 1) * kn]
                            i0 = prev.rearrange("p (k l) -> p k l", k=KH)[:, c * kn:(c + 1) * kn].unsqueeze(2)\
                                     .to_broadcast([P, kn, 2, 1 << stage])
                            i1 = ps[bank + c][:, col:col + n // kb].rearrange("p (k a l) -> p k a l", k=kn, a=2)
                            last = nc.vector.tensor_tensor(out=o, in0=i0, in1=i1, op=ALU.mult)
                        last.then_inc(low_product, 1)
                    prev = cur

            low_matrix(X_up, 0)
            low_matrix(X_dn, 1)
            for i in range(KH + 2):
                if i < KH and i % 2 == 1:
                    dve.wait_ge(wt_turned, i + 1)
                    nc.vector.tensor_copy(Y[:, i, :], ps[5][:, :]).then_inc(wt_kept[1], 1)
                k = i - 2
                if k >= 0 and k % 2 == 1:
                    dve.wait_ge(low_mixed, k + 1)
                    nc.vector.tensor_copy(Y[:, k, :], ps[k % 4][:, :]).then_inc(low_kept[1], 1)

            def high_sums(plan, buf, coef, dn):
                for q, (bit, m, a, b, wa, wb) in enumerate(plan):
                    dve.wait_ge(scaled[dn], 2 * q + 2)
                    wait(dve, mixed[dn], wb)
                    if not dn and bit == 0:
                        dve.wait_ge(low_kept[1], b // 2 + 1)
                    for o, dst in enumerate((a, b)):
                        e = 2 + o if dn else 2 * o + 1
                        nc.vector.scalar_tensor_tensor(out=buf[:, dst, :], in0=buf[:, b, :],
                                                       scalar=coef[:, bit, m, e:e + 1],
                                                       in1=tmp[:, (2 * q + o) % 8, :],
                                                       op0=ALU.mult, op1=ALU.add).then_inc(mixed[dn], 1)

            dve.wait_ge(coef_loaded, 2 * NX)
            high_sums(up_plan, Y, hc_up, 0)
            for i, k in enumerate(W1_ORDER):
                dve.wait_ge(w1hi_ready, i + 1)
                nc.vector.tensor_tensor(out=W1lo[:, k, :, :].rearrange("p c h -> p (c h)"), in0=ps[i % 4][:, :],
                                        in1=W1hi[:, k, :, :].rearrange("p c h -> p (c h)").bitcast(f32),
                                        op=ALU.subtract).then_inc(w1lo_ready, 1)
            dve.wait_ge(bias_loaded, 4 * NX)
            nc.vector.tensor_tensor(out=bias_row[:, :], in0=bias_row[:, :], in1=bias_tmp, op=ALU.add)\
                .then_inc(bias_row_ready, 1)
            dve.wait_ge(wcon_loaded, KH // 4 * NX)
            high_sums(dn_plan, wcon, hc_dn, 1)
            for i, k in enumerate(W2_ORDER):
                dve.wait_ge(w2hi_ready, i + 1)
                nc.vector.tensor_tensor(out=W2lo[:, k, :], in0=ps[4 + i % 4][:, :], in1=W2hi[:, k, :].bitcast(f32),
                                        op=ALU.subtract).then_inc(w2lo_ready, 1)

            def scan_chunk(u, j):
                n = u * J + j
                if j == 0:
                    dve.wait_ge(squared, u + 1)
                wait(dve, gate_turned, n)
                nc.vector.transpose(kvT[:, :, :].rearrange("p b i -> p (b i)"), kv[:, j, :]).then_inc(kv_turned, 1)
                dve.wait_ge(kv_turned, n + 1)
                dve.wait_ge(carry_saved, n + 1)
                nc.vector.scalar_tensor_tensor(out=kvT[:, :, 0], in0=carry[:, :], scalar=DECAY, in1=kvT[:, :, 0],
                                               op0=ALU.mult, op1=ALU.add).then_inc(carry_added, 1)
                dve.wait_ge(carry_added, n + 1)
                flat = kvT[:, :, :].rearrange("p b i -> p (b i)")
                nc.vector.tensor_tensor_scan(out=flat, data0=decay[:, :], data1=flat, initial=0.0,
                                             op0=ALU.mult, op1=ALU.add).then_inc(scanned, 1)
                dve.wait_ge(scanned, n + 1)
                if j < J - 1:
                    nc.vector.tensor_copy(carry[:, :], kvT[:, :, Q - 1]).then_inc(carry_saved, 1)
                else:
                    nc.vector.tensor_scalar(carry[:, :].bitcast(i32), kvT[:, :, Q - 1].bitcast(i32),
                                            keep[:, bass.ds(u, 1)], None, ALU.bitwise_and).then_inc(carry_saved, 1)
                nc.vector.transpose(kv[:, j, :], flat).then_inc(gate_turned, 1)

            def stats1(u, x):
                dve.wait_ge(x_loaded, (u + 1) * (G * NX))
                for j in range(J):
                    nc.vector.bn_stats(st1[:, j, :], x[:, j, :]).then_inc(stats1_done, 1)
                dve.wait_ge(stats1_done, u * J + J)
                nc.vector.memset(wait_pad[:, J:J + 1], 0.0)
                for j in range(J):
                    nc.vector.bn_aggr(mv1[:, j, :], st1[:, j, :]).then_inc(mean1_ready, 1)

            def gate(u, x, j):
                n = u * J + j
                if j == 0:
                    dve.wait_ge(rstd1_ready, u + 1)
                    dve.wait_ge(gate_turned, u * J + J)
                    dve.wait_ge(mean1_ready, u * J + J)
                nc.vector.scalar_tensor_tensor(out=kv[:, j, :], in0=x[:, j, :], scalar=mv1[:, j, 0:1], in1=kv[:, j, :],
                                               op0=ALU.subtract, op1=ALU.mult).then_inc(gated, 1)
                dve.wait_ge(gated, n + 1)
                nc.vector.scalar_tensor_tensor(out=x[:, j, :], in0=kv[:, j, :], scalar=rstd1[:, j:j + 1],
                                               in1=x[:, j, :], op0=ALU.mult, op1=ALU.add).then_inc(x1_ready, 1)
                dve.wait_ge(x1_ready, n + 1)
                nc.vector.bn_stats(st2[:, j, :], x[:, j, :]).then_inc(stats2_done, 1)
                dve.wait_ge(stats2_done, n + 1)
                nc.vector.memset(wait_pad[:, j:j + 1], 0.0)
                nc.vector.bn_aggr(mv2[:, j, :], st2[:, j, :]).then_inc(mean2_ready, 1)

            def normalise(u, x, j):
                n = u * J + j
                dve.wait_ge(rstd2_ready, n + 1)
                dve.wait_ge(mean2_ready, n + 1)
                nc.vector.tensor_scalar(kv[:, j, :], x[:, j, :], mv2[:, j, 0:1], rstd2[:, j:j + 1],
                                        ALU.subtract, ALU.mult).then_inc(xn_ready, 1)
                dve.wait_ge(xn_ready, n + 1)
                nc.vector.tensor_tensor(out=x[:, j, :], in0=x[:, j, :], in1=bias_row[:, :], op=ALU.add)\
                    .then_inc(bias_added, 1)

            def keep_xT_lo(u, par, j):
                dve.wait_ge(xThi_ready, u * J + j + 1)
                hi = xThi[par][:, :, j * P:(j + 1) * P].bitcast(f32)
                nc.vector.tensor_tensor(out=xTlo[par][:, :, j * P:(j + 1) * P],
                                        in0=ps_t[j % 2][:, :].rearrange("p (c n) -> p c n", c=KD), in1=hi,
                                        op=ALU.subtract).then_inc(xTlo_ready, 1)

            dve.wait_ge(const_ready, 2)
            dve.wait_ge(bias_row_ready, 1)
            for j in range(J):
                scan_chunk(0, j)
            stats1(0, xs[0])
            for j in range(J):
                gate(0, xs[0], j)
            for j in range(J):
                normalise(0, xs[0], j)
                keep_xT_lo(0, 0, j)

            def finish(t, par, j):
                nc.vector.tensor_tensor(out=xs[par][:, j, :], in0=ps_y[j][:, :], in1=xs[par][:, j, :], op=ALU.add)\
                    .then_inc(out_ready, 1)

            def finish_step(t, par):
                dve.wait_ge(y_part, (t + 1) * KH)
                dve.wait_ge(bias_added, (t + 1) * J)
                for j in range(J):
                    finish(t, par, j)

            def body(t, par, first, last):
                nxt = xs[1 - par]
                for k in range(KH):
                    s = t * KH + k
                    slot = k % 2
                    dve.wait_ge(gelu_ready, s + 1)
                    wait(dve, y_part, s - 1)
                    nc.vector.tensor_copy(ghi[:, slot, :], g32[:, slot, :]).then_inc(ghi_ready, 1)
                    dve.wait_ge(ghi_ready, s + 1)
                    nc.vector.tensor_tensor(out=glo[:, slot, :], in0=g32[:, slot, :],
                                            in1=ghi[:, slot, :].bitcast(f32), op=ALU.subtract).then_inc(glo_ready, 1)
                    if k == LAG - 1 and not first:
                        finish_step(t - 1, 1 - par)
                    if last:
                        continue
                    u = t + 1
                    if 2 <= k < 2 + J:
                        scan_chunk(u, k - 2)
                    if k == 6:
                        stats1(u, nxt)
                    if 7 <= k < 7 + J:
                        gate(u, nxt, k - 7)
                    if 8 <= k < 8 + J:
                        normalise(u, nxt, k - 8)
                    if 10 <= k < 10 + J:
                        keep_xT_lo(u, 1 - par, k - 10)

            steps(dve, body)
            finish_step(T - 1, (T - 1) % 2)

        @block.tensor
        def _(pe):
            pe.wait_ge(ident_ready, 1)
            pe.wait_ge(sel_ready, 2 * LOW)

            def spread(src, dn):
                pe.wait_ge(low_loaded[dn], LOW * NX)
                if dn:
                    pe.wait_ge(low_product, LOW)
                for stage in range(LOW):
                    rows, off, n_src = low_src(stage)
                    bank, col = spread_place(stage)
                    n = KH << (stage + 1)
                    kb = max(1, n // 512)
                    kn = KH // kb
                    v = src[0:rows, off:off + n_src].rearrange("q (k l a b) -> q k a l b", k=KH, a=2, b=2)
                    for c in range(kb):
                        for bit in range(2):
                            last = nc.tensor.matmul(ps[bank + c][:, col:col + n // kb], sel[0:rows, stage, bit, :],
                                                    v[:, c * kn:(c + 1) * kn, :, :, bit],
                                                    start=(bit == 0), stop=(bit == 1))
                    last.then_inc(coef_spread, 1)

            spread(lowsrc_up, 0)
            spread(lowsrc_dn, 1)
            pe.wait_ge(low_product, 2 * LOW)
            pe.wait_ge(bias_loaded, 4 * NX)
            nc.tensor.transpose(ps[6][:, 0:2 * KH], bias_rows, ident[0:2 * KH, 0:2 * KH]).then_inc(bcol_turned, 1)
            for q in range(KH // 4):
                for i in range(4):
                    last = nc.tensor.transpose(ps[q][:, i * P:(i + 1) * P], X_dn[:, 4 * q + i, :], ident[:, :])
                last.then_inc(dn_turned, 1)
            pe.wait_ge(wexp_loaded, KD * NX)
            for i in range(KH + 2):
                if i < KH:
                    wait(pe, wt_kept[i % 2], i // 2)
                    for c in range(KD):
                        last = nc.tensor.transpose(ps[4 + i % 2][:, c * P:(c + 1) * P], wexp[:, c, i * P:(i + 1) * P],
                                                   ident[:, :])
                    last.then_inc(wt_turned, 1)
                k = i - 2
                if k >= 0:
                    pe.wait_ge(wt_kept[k % 2], k // 2 + 1)
                    if k < 4:
                        pe.wait_ge(dn_kept, k + 1)
                    else:
                        pe.wait_ge(low_kept[k % 2], (k - 4) // 2 + 1)
                    nc.tensor.matmul(ps[k % 4][:, :], X_up[:, k, :], Y[:, k, :], start=True, stop=True)\
                        .then_inc(low_mixed, 1)
            pe.wait_ge(bcol_kept, 1)
            for k in range(KH):
                last = nc.tensor.matmul(ps[7][:, k:k + 1], X_up[:, k, :], bcol[:, k:k + 1], start=True, stop=True)
            last.then_inc(bias_low, 1)
            for i, k in enumerate(W1_ORDER):
                pe.wait_ge(mixed[0], up_written[k])
                if i < 4:
                    pe.wait_ge(low_kept[i % 2], KH // 2)
                else:
                    pe.wait_ge(w1lo_ready, i - 3)
                for c in range(KD):
                    last = nc.tensor.transpose(ps[i % 4][:, c * P:(c + 1) * P], Y[:, k, c * P:(c + 1) * P], ident[:, :])
                last.then_inc(w1_turned, 1)
            pe.wait_ge(dn_kept, KH // 4)
            pe.wait_ge(yb_kept, 1)
            for i, k in enumerate(W2_ORDER):
                pe.wait_ge(mixed[1], dn_written[k])
                wait(pe, w2lo_ready, i - 3)
                nc.tensor.matmul(ps[4 + i % 4][:, :], X_dn[:, k, :], wcon[:, k, :], start=True, stop=True)\
                    .then_inc(w2_mixed, 1)

            def turn_x(u, j):
                n = u * J + j
                pe.wait_ge(xn_ready, n + 1)
                wait(pe, xTlo_ready, n - 1)
                for c in range(KD):
                    last = nc.tensor.transpose(ps_t[j % 2][:, c * P:(c + 1) * P], kv[:, j, c * P:(c + 1) * P], ident[:, :])
                last.then_inc(xT_turned, 1)

            pe.wait_ge(w1lo_ready, KH)
            for j in range(J):
                turn_x(0, j)
            pe.wait_ge(w2lo_ready, KH)

            def up_product(t, par, k):
                s = t * KH + k
                if k == 0:
                    pe.wait_ge(xTlo_ready, (t + 1) * J)
                wait(pe, gelu_ready, s - 1)
                terms = [(w, v) for c in range(KD) for w, v in
                         ((W1hi[:, k, c, :], xThi[par][:, c, :]), (W1hi[:, k, c, :], xTlo[par][:, c, :]),
                          (W1lo[:, k, c, :], xThi[par][:, c, :]))]
                for i, (w, v) in enumerate(terms):
                    last = nc.tensor.matmul(ps_h[k % 2][:, :], w, v, start=(i == 0), stop=(i == len(terms) - 1))
                last.then_inc(h_ready, 1)

            def down_product(t, k, first):
                s = t * KH + k
                pe.wait_ge(glo_ready, s + 1)
                for j in range(J):
                    if k == 0 and not first:
                        pe.wait_ge(out_ready, (t - 1) * J + (j + 1))
                    tok = slice(j * P, (j + 1) * P)
                    for i, (g, w) in enumerate(((ghi, W2hi), (ghi, W2lo), (glo, W2hi))):
                        last = nc.tensor.matmul(ps_y[j][:, :], g[:, k % 2, tok], w[:, k, :],
                                                start=(k == 0 and i == 0), stop=(k == KH - 1 and i == 2))
                last.then_inc(y_part, 1)

            def body(t, par, first, last):
                for k in range(KH):
                    up_product(t, par, k)
                    if k >= LAG:
                        down_product(t, k - LAG, first)
                    elif not first:
                        down_product(t - 1, k - LAG + KH, False)
                    if not last and 9 <= k < 9 + J:
                        turn_x(t + 1, k - 9)

            steps(pe, body)
            for k in range(KH - LAG, KH):
                down_product(T - 1, k, False)


_INS = ['x', 'ctx_1024', 'L0_ffn_W_exp', 'L0_ffn_b_exp', 'L0_ffn_up_weights', 'L0_ffn_up_bias',
        'L0_ffn_down_weights', 'L0_ffn_W_con', 'L0_ffn_b_con', 'L0_ffn_down_bias']


def kernel(**inputs):
    import numpy as _np
    import concourse.bacc as _bacc
    from concourse import mybir as _mybir
    from concourse.bass_utils import run_bass_kernel_spmd as _run

    nc = _bacc.Bacc("TRN2", target_bir_lowering=False, num_devices=1)
    arrays, args = {}, []
    for name in _INS:
        a = _np.ascontiguousarray(inputs[name])
        arrays[f"in_{name}_dram"] = a
        args.append(nc.dram_tensor(f"in_{name}_dram", a.shape, _mybir.dt.from_np(a.dtype), kind="ExternalInput").ap())
    shape = inputs['x'].shape
    args.append(nc.dram_tensor("out_dram", shape, _mybir.dt.float32, kind="ExternalOutput").ap())
    xattn_ffn_program(nc, *args)
    r = _run(nc, [arrays], core_ids=[0])
    return r.results[0]["out_dram"]
```

```python
import concourse.bass as bass
from concourse import mybir
from contextlib import ExitStack


def xattn_ffn_program(nc, x_in, ctx_in, w_exp, b_exp, up_w, up_bias, down_w, w_con, b_con, down_bias, out):
    f32 = mybir.dt.float32
    f32r = mybir.dt.float32r
    i32 = mybir.dt.int32
    ALU = mybir.AluOpType
    ACT = mybir.ActivationFunctionType

    P = 128
    B, S, D = x_in.shape
    H = w_exp.shape[1]
    KD = D // P
    KH = H // P
    LOW = 7
    HIGH = up_w.shape[0] - LOW
    PAIRS = KH // 2
    E = P // KH
    R = P // E
    G = 4
    Q = 32
    J = 4
    T = B * S // (J * P)
    STEPS_PER_BATCH = S // (Q * J)
    DECAY = 0.9
    EPS = 1e-5
    LAG = 2
    NX = 16

    def token_rows(a):
        return a.rearrange("b s d -> (b s) d").rearrange("(g t j i) d -> g t i j d", g=G, t=T, j=J, i=Q)

    x_rows, ctx_rows, out_rows = token_rows(x_in), token_rows(ctx_in), token_rows(out)

    es = ExitStack()
    with es:
        def sb(name, shape, dt=f32, stack=es):
            return stack.enter_context(nc.sbuf_tensor(name, shape, dt))

        def sem(name):
            return es.enter_context(nc.semaphore(name))

        fold = ExitStack()
        wexp = sb("wexp", [P, KD, H], stack=fold)
        WT = sb("WT", [P, KH, D], stack=fold)
        wcon = sb("wcon", [P, KH, D], stack=fold)
        Z = sb("Z", [P, KH, D], stack=fold)
        HX = sb("HX", [P, 2, R, P], stack=fold)
        LX = sb("LX", [P, 2, KH, P], stack=fold)
        half = sb("half", [P, KH * P // 2], stack=fold)
        sel = sb("sel", [P, LOW, 2, P], stack=fold)
        fold.close()
        W1hi = sb("W1hi", [P, KH, KD, P], f32r)
        W1lo = sb("W1lo", [P, KH, KD, P], f32r)
        W2hi = sb("W2hi", [P, KH, D], f32r)
        W2lo = sb("W2lo", [P, KH, D], f32r)
        xThi, xTlo = [], []
        for par in range(2):
            xThi.append(sb(f"xThi{par}", [P, KD, J * P], f32r))
            xTlo.append(sb(f"xTlo{par}", [P, KD, J * P], f32r))
        g32 = sb("g32", [P, 2, J * P])
        ghi = sb("ghi", [P, 2, J * P], f32r)
        glo = sb("glo", [P, 2, J * P], f32r)
        xs = [sb(f"x{par}", [P, J, D]) for par in range(2)]
        kv = sb("kv", [P, J, D])
        kvT = sb("kvT", [P, D // Q, Q])
        decay = sb("decay", [P, D])
        bias_row = sb("bias_row", [P, D])
        ident = sb("ident", [P, P])
        carry = sb("carry", [P, D // Q])
        keep = sb("keep", [P, T + 1], i32)
        st1 = sb("st1", [P, J, 6])
        mv1 = sb("mv1", [P, J, 2])
        ve1 = sb("ve1", [P, J])
        rstd1 = sb("rstd1", [P, J])
        st2 = sb("st2", [P, J, 6])
        mv2 = sb("mv2", [P, J, 2])
        ve2 = sb("ve2", [P, J])
        rstd2 = sb("rstd2", [P, J])
        neg_half = sb("neg_half", [P, J])
        wait_pad = sb("wait_pad", [P, J + 1])
        eps = sb("eps", [P, J])
        gelu_bias = sb("gelu_bias", [P, KH])
        flat1 = xs[1][:, :, :].rearrange("p j d -> p (j d)")
        hc_up = flat1[:, 0:HIGH * PAIRS * 4].rearrange("p (s m e) -> p s m e", s=HIGH, m=PAIRS)
        same_e = flat1[:, 128:128 + E]
        bias_rows = flat1[0:2 * KH, 256:256 + P]
        bcol = flat1[:, 384:384 + 2 * KH]
        yb = flat1[:, 448:448 + KH]
        ybt = flat1[:, 512:512 + 4 * PAIRS].rearrange("p (e m) -> p e m", e=4)
        high_half = flat1[:, 640:640 + R * KH // 2]
        high_full = flat1[:, 768:768 + R * KH]
        bias_tmp = flat1[:, 1024:1024 + D]

        def flat(a):
            return a.rearrange("p a b -> p (a b)")
        low_src = [flat(Z[:, 0:8, :]), flat(wcon[:, 0:8, :])]
        top_src = [flat(Z[:, 8:16, :]), flat(wcon[:, 8:16, :])]
        high_src = [flat(HX[:, 1, 0:8, :]), flat(HX[:, 1, 8:16, :])]

        ps = [es.enter_context(nc.psum_tensor(f"ps{i}", [P, 512], f32)) for i in range(8)]
        ps_h, ps_t, ps_y = ps[0:2], ps[2:4], ps[4:8]
        ps_f = ps[5:8]

        low_loaded = [sem("low_up_loaded"), sem("low_dn_loaded")]
        top_loaded = [sem("top_up_loaded"), sem("top_dn_loaded")]
        coef_loaded = sem("coef_loaded")
        bias_loaded = sem("bias_loaded")
        wexp_loaded = [sem(f"wexp_loaded{c}") for c in range(4)]
        wcon_loaded = [sem("wcon_low_loaded"), sem("wcon_high_loaded")]
        x_loaded = sem("x_loaded")
        ctx_loaded = sem("ctx_loaded")
        out_stored = sem("out_stored")
        ident_zero = sem("ident_zero")
        ident_ready = sem("ident_ready")
        sel_zero = sem("sel_zero")
        sel_ready = sem("sel_ready")
        const_ready = sem("const_ready")
        const_base = sem("const_base")
        neg_ready = sem("neg_ready")
        mask_ready = sem("mask_ready")
        coef_spread = sem("coef_spread")
        path_product = sem("path_product")
        low_matrix_ready = sem("low_matrix_ready")
        high_matrix_ready = sem("high_matrix_ready")
        bcol_turned = sem("bcol_turned")
        bcol_kept = sem("bcol_kept")
        bias_low = sem("bias_low")
        yb_kept = sem("yb_kept")
        yb_step = sem("yb_step")
        gelu_bias_ready = sem("gelu_bias_ready")
        fold_made = sem("fold_made")
        fold_kept = {"act": sem("fold_kept_act"), "dve": sem("fold_kept_dve")}
        hi_split = sem("hi_split")
        bias_row_ready = sem("bias_row_ready")
        high_loaded = [sem("high_up_loaded"), sem("high_dn_loaded")]
        HIGH_LOADS = KH - 1

        squared = sem("squared")
        kv_turned = sem("kv_turned")
        carry_added = sem("carry_added")
        scanned = sem("scanned")
        carry_saved = sem("carry_saved")
        gate_turned = sem("gate_turned")
        stats1_done = sem("stats1_done")
        mean1_ready = sem("mean1_ready")
        eps1_added = sem("eps1_added")
        rstd1_ready = sem("rstd1_ready")
        gated = sem("gated")
        x1_ready = sem("x1_ready")
        stats2_done = sem("stats2_done")
        mean2_ready = sem("mean2_ready")
        eps2_added = sem("eps2_added")
        rstd2_ready = sem("rstd2_ready")
        xn_ready = sem("xn_ready")
        bias_added = sem("bias_added")
        xT_turned = sem("xT_turned")
        xThi_ready = sem("xThi_ready")
        xTlo_ready = sem("xTlo_ready")
        h_ready = sem("h_ready")
        gelu_ready = sem("gelu_ready")
        ghi_ready = sem("ghi_ready")
        glo_ready = sem("glo_ready")
        y_part = sem("y_part")
        out_ready = sem("out_ready")

        def wait(eng, semaphore, value):
            if isinstance(value, int) and value <= 0:
                return
            eng.wait_ge(semaphore, value)

        block = es.enter_context(nc.Block())

        def steps(eng, body):
            body(0, 0, first=True, last=False)
            with eng.Fori(1, T - 1, 2) as t:
                body(t, 1, first=False, last=False)
                body(t + 1, 0, first=False, last=False)
            body(T - 1, (T - 1) % 2, first=False, last=True)

        FOLD = [("WT", k, "act") for k in range(KH)]
        FOLD += [("low_up", k, "act") for k in range(KH)]
        FOLD += [("regroup", r, "act") for r in range(R)]
        FOLD += [("high_up", r, "split") for r in range(R)]
        FOLD += [("turn_high", q, ("act", "dve")[q % 2]) for q in range(R // 4)]
        FOLD += [("high_dn", r, ("act", "dve")[r % 2]) for r in range(R)]
        FOLD += [("turn_low", q, ("act", "dve")[q % 2]) for q in range(KH // 4)]
        FOLD += [("back", k, ("act", "dve")[k % 2]) for k in range(KH)]
        FOLD += [("low_dn", k, "split") for k in range(KH)]

        kept_count, kept_so_far = [], {"act": 0, "dve": 0}
        for _, _, who in FOLD:
            who = "dve" if who == "split" else who
            kept_so_far[who] += 1
            kept_count.append((who, kept_so_far[who]))

        def wait_kept(eng, kind, i):
            who, count = kept_count[fold_at(kind, i)]
            eng.wait_ge(fold_kept[who], count)

        def fold_at(kind, i):
            return [(a, b) for a, b, _ in FOLD].index((kind, i))

        def src_place(stage):
            n = 4 * KH << stage
            return (P // 2) >> stage, n - 4 * KH, n

        LOW_PLACE = [(0, 448), (0, 384), (0, 256), (0, 0), (1, 0), (2, 0)]
        HIGH_PLACE = [(4, 448), (4, 384), (4, 256), (4, 0)]
        LOWS = LOW - 1
        def spreads(dn, stage):
            return dn * (LOWS + HIGH) + stage + 1
        UP_DONE = LOWS + HIGH
        ALL_DONE = 2 * UP_DONE

        def path_stage(eng, cur, prev, coef, stage):
            lanes, outer = coef.shape[0], coef.shape[1]
            return eng.tensor_tensor(out=cur.rearrange("p (o a l) -> p o a l", o=outer, a=2),
                                     in0=prev.rearrange("p (o l) -> p o l", o=outer).unsqueeze(2)
                                     .to_broadcast([lanes, outer, 2, 1 << stage]), in1=coef, op=ALU.mult)

        def top_stage(eng, dn):
            src = top_src[dn].rearrange("p (o l a b) -> p o a l b", o=KH, a=2, b=2)
            for bit in range(2):
                lanes = slice(bit * P // 2, (bit + 1) * P // 2)
                last = path_stage(eng, flat(LX[:, dn, :, :])[lanes], half[lanes], src[lanes, :, :, :, bit], LOW - 1)
            return last

        def columns(bank):
            return bank[:, :].rearrange("p (c e k) -> p c e k", c=KD, e=E)

        def w1_columns(w, r):
            return w[:, :, :, r:P:R].rearrange("p k c e -> p c e k")

        def spread_columns(a, r):
            return a[:, :, r:H:R].rearrange("p c (k e) -> p c e k", e=E)

        Zd = Z[:, :, :].rearrange("p a b -> p (a b)").rearrange("p (c h) -> p c h", c=KD)

        def kept(kind, i, bank):
            whole = bank[:, :]
            if kind == "WT":
                return WT[:, i, :], whole
            if kind == "low_up":
                return wexp[:, :, i:H:KH].rearrange("p c (r e) -> p c e r", e=E),\
                    whole.rearrange("p (c e r) -> p c e r", c=KD, e=E)
            if kind == "regroup":
                return Z[:, i, :], whole
            if kind == "turn_high":
                return HX[:, 1, 4 * i:4 * i + 4, :].rearrange("p a b -> p (a b)"), whole
            if kind == "high_dn":
                return spread_columns(Zd, i), columns(bank)
            if kind == "turn_low":
                return LX[:, 1, 4 * i:4 * i + 4, :].rearrange("p a b -> p (a b)"), whole
            assert kind == "back"
            return wcon[:, i, :], whole

        @block.sync
        def _(sp):
            def load_tokens(dst, rows, t, loaded):
                for g in range(G):
                    sp.dma_start(dst[Q * g:Q * g + Q, :, :], rows[g, t]).then_inc(loaded, NX)

            def load_coefs(weights, dn):
                for stage in range(LOWS):
                    rows, off, n = src_place(stage)
                    src = weights[stage].rearrange("(k q l) a b -> q k (l a b)", k=KH, q=rows)
                    sp.dma_start(low_src[dn][0:rows, off:off + n].rearrange("q (k n) -> q k n", k=KH), src)\
                      .then_inc(low_loaded[dn], NX)

            def load_top(weights, dn):
                sp.dma_start(top_src[dn], weights[LOW - 1].rearrange("m a b -> (m a b)").partition_broadcast(P))\
                  .then_inc(top_loaded[dn], NX)

            load_coefs(up_w, 0)
            wexp_src = w_exp.rearrange("(c p) h -> p c h", p=P)
            for q in range(4):
                part = slice(q * H // 4, (q + 1) * H // 4)
                sp.dma_start(wexp[:, :, part], wexp_src[:, :, part]).then_inc(wexp_loaded[q], NX)
            load_top(up_w, 0)
            load_tokens(kv, ctx_rows, 0, ctx_loaded)
            load_tokens(xs[0], x_rows, 0, x_loaded)
            load_coefs(down_w, 1)
            load_top(down_w, 1)
            wcon_src = w_con.rearrange("(k e r) d -> e k (r d)", e=E, r=R)
            for part in range(2):
                if part == 0:
                    sp.wait_ge(coef_spread, ALL_DONE)
                else:
                    sp.wait_ge(low_matrix_ready, 2)
                cols = slice(part * R * D // 2, (part + 1) * R * D // 2)
                for e in range(E):
                    sp.dma_start(flat(wcon[KH * e:KH * (e + 1), :, :])[:, cols], wcon_src[e][:, cols])\
                      .then_inc(wcon_loaded[part], NX)
            sp.wait_ge(xT_turned, J)
            load_tokens(kv, ctx_rows, 1, ctx_loaded)

            def body(t, par, first, last):
                if first:
                    sp.wait_ge(high_matrix_ready, 2)
                    sp.wait_ge(bias_row_ready, 1)
                    sp.wait_ge(gelu_bias_ready, 1)
                else:
                    sp.wait_ge(out_ready, t * J)
                    for g in range(G):
                        sp.dma_start(out_rows[g, t - 1], xs[1 - par][Q * g:Q * g + Q, :, :])\
                          .then_inc(out_stored, NX)
                if not last:
                    if not first:
                        sp.wait_ge(out_stored, t * (G * NX))
                    load_tokens(xs[1 - par], x_rows, t + 1, x_loaded)

            def next_ctx(t):
                sp.wait_ge(xT_turned, (t + 2) * J)
                load_tokens(kv, ctx_rows, t + 2, ctx_loaded)

            body(0, 0, True, False)
            next_ctx(0)
            with sp.Fori(1, T - 3, 2) as t:
                body(t, 1, False, False)
                next_ctx(t)
                body(t + 1, 0, False, False)
                next_ctx(t + 1)
            body(T - 3, (T - 3) % 2, False, False)
            next_ctx(T - 3)
            body(T - 2, (T - 2) % 2, False, False)
            body(T - 1, (T - 1) % 2, False, True)
            sp.wait_ge(out_ready, T * J)
            for g in range(G):
                sp.dma_start(out_rows[g, T - 1], xs[(T - 1) % 2][Q * g:Q * g + Q, :, :]).then_inc(out_stored, NX)
            sp.wait_ge(out_stored, T * G * NX)

        @block.gpsimd
        def _(pool):
            nc.gpsimd.memset(ident[:, :], 0.0).then_inc(ident_zero, 1)
            nc.gpsimd.memset(sel[:, :, :, :], 0.0).then_inc(sel_zero, 1)
            pool.wait_ge(ident_zero, 1)
            nc.gpsimd.affine_select(out=ident[:, :], in_=ident[:, :], compare_op=ALU.not_equal, fill=1.0, base=0,
                                    pattern=[[-1, P]], channel_multiplier=1).then_inc(ident_ready, 1)
            pool.wait_ge(sel_zero, 1)
            for stage in range(LOW):
                rows = (P // 2) >> stage
                for bit in range(2):
                    v = sel[0:rows, stage, bit, :].rearrange("q (a b) -> q a b", b=1 << stage)
                    nc.gpsimd.affine_select(out=v, in_=v, compare_op=ALU.not_equal, fill=1.0, base=bit,
                                            pattern=[[-1, P >> stage], [0, 1 << stage]], channel_multiplier=2)\
                        .then_inc(sel_ready, 1)
            nc.gpsimd.memset(neg_half[:, :], -0.5).then_inc(neg_ready, 1)
            nc.gpsimd.memset(eps[:, :], EPS).then_inc(neg_ready, 1)

            def high_matrix(dn):
                pool.wait_ge(path_product, ALL_DONE if dn else UP_DONE)
                pool.wait_ge(mask_ready, 1)
                if dn:
                    pool.wait_ge(coef_spread, ALL_DONE)
                nc.gpsimd.tensor_tensor(
                    out=HX[:, dn, :, :].rearrange("p r (e k) -> p r e k", e=E),
                    in0=high_full.rearrange("p (r k) -> p r k", r=R).unsqueeze(2).to_broadcast([P, R, E, KH]),
                    in1=same_e.unsqueeze(1).unsqueeze(3).to_broadcast([P, R, E, KH]), op=ALU.mult)\
                    .then_inc(high_matrix_ready, 1)

            def rstd(u):
                pool.wait_ge(mean1_ready, u * J + J)
                nc.gpsimd.tensor_tensor(out=ve1[:, :], in0=mv1[:, :, 1], in1=eps[:, :], op=ALU.add).then_inc(eps1_added, 1)
                pool.wait_ge(eps1_added, u + 1)
                nc.gpsimd.tensor_tensor(out=rstd1[:, :], in0=ve1[:, :], in1=neg_half[:, :], op=ALU.pow)\
                    .then_inc(rstd1_ready, 1)
                for j in range(J):
                    pool.wait_ge(mean2_ready, u * J + j + 1)
                    nc.gpsimd.tensor_tensor(out=ve2[:, j:j + 1], in0=mv2[:, j, 1:2], in1=eps[:, j:j + 1], op=ALU.add)\
                        .then_inc(eps2_added, 1)
                    pool.wait_ge(eps2_added, u * J + j + 1)
                    nc.gpsimd.tensor_tensor(out=rstd2[:, j:j + 1], in0=ve2[:, j:j + 1], in1=neg_half[:, j:j + 1],
                                            op=ALU.pow).then_inc(rstd2_ready, 1)

            high_matrix(0)
            pool.wait_ge(neg_ready, 2)
            rstd(0)
            pool.wait_ge(path_product, spreads(1, LOW - 2))
            pool.wait_ge(low_matrix_ready, 1)
            pool.wait_ge(top_loaded[1], NX)
            top_stage(nc.gpsimd, 1).then_inc(low_matrix_ready, 1)
            pool.wait_ge(low_matrix_ready, 2)
            high_matrix(1)

            pool.wait_ge(coef_loaded, NX)
            pool.wait_ge(yb_kept, 1)
            n = 0

            def step(ins):
                nonlocal n
                n += 1
                ins.then_inc(yb_step, 1)

            for bit in range(HIGH):
                v = yb.rearrange("p (h s l) -> p h s l", s=2, l=1 << bit)
                c = hc_up[:, bit, :, :].rearrange("p (h l) e -> p h l e", l=1 << bit)
                tt = ybt.rearrange("p e (h l) -> p e h l", l=1 << bit)
                if n:
                    pool.wait_ge(yb_step, n)
                for e in range(4):
                    step(nc.gpsimd.tensor_tensor(out=tt[:, e], in0=v[:, :, e % 2, :], in1=c[:, :, :, e], op=ALU.mult))
                pool.wait_ge(yb_step, n)
                for o in range(2):
                    step(nc.gpsimd.tensor_tensor(out=v[:, :, o, :], in0=tt[:, 2 * o], in1=tt[:, 2 * o + 1], op=ALU.add))
            pool.wait_ge(yb_step, n)
            nc.gpsimd.tensor_tensor(out=gelu_bias[:, :], in0=yb, in1=bcol[:, KH:2 * KH], op=ALU.add)\
                .then_inc(gelu_bias_ready, 1)

            with pool.Fori(1, T) as u:
                rstd(u)

        @block.scalar
        def _(act):
            def load_high(weights, dn):
                count = 0
                for b in range(HIGH):
                    rows, off, n = src_place(b)
                    top = KH >> (b + 1)
                    src = weights[LOW + b].rearrange("(i l e n) x y -> i e l (n x y)", i=top, e=E, n=R)
                    dst = high_src[dn][0:rows, off:off + n].rearrange("q (l n) -> q l n", l=1 << b)
                    for i in range(top):
                        act.dma_start(dst[i:rows:top], src[i]).then_inc(high_loaded[dn], NX)
                        count += 1
                return count

            load_high(up_w, 0)
            act.dma_start(bias_rows[0:KH, :], b_exp.rearrange("(k p) -> k p", p=P)).then_inc(bias_loaded, NX)
            act.dma_start(bias_rows[KH:2 * KH, :], up_bias.rearrange("(k p) -> k p", p=P)).then_inc(bias_loaded, NX)
            act.dma_start(hc_up, up_w[LOW:LOW + HIGH].rearrange("s (m p) a b -> p s m (a b)", p=P))\
               .then_inc(coef_loaded, NX)
            load_high(down_w, 1)
            act.dma_start(bias_row[:, :], b_con.partition_broadcast(P)).then_inc(bias_loaded, NX)
            act.dma_start(bias_tmp, down_bias.partition_broadcast(P)).then_inc(bias_loaded, NX)

            def fold_step(kind, i):
                n = fold_at(kind, i)
                bank = ps_f[n % 3]
                act.wait_ge(fold_made, n + 1)
                if kind == "high_up":
                    act.activation(w1_columns(W1hi, i), columns(bank), ACT.Copy).then_inc(hi_split, 1)
                elif kind == "low_dn":
                    act.activation(W2hi[:, i, :], bank[:, :], ACT.Copy).then_inc(hi_split, 1)
                elif FOLD[n][2] == "act":
                    act.activation(*kept(kind, i, bank), ACT.Copy).then_inc(fold_kept["act"], 1)

            def square(u):
                act.wait_ge(ctx_loaded, (u + 1) * (G * NX))
                act.activation(kv[:, :, :], kv[:, :, :], ACT.Square).then_inc(squared, 1)

            for k in range(KH):
                fold_step("WT", k)
            square(0)
            for k in range(KH):
                fold_step("low_up", k)
            def keep_xT_hi(u, par, j):
                act.wait_ge(xT_turned, u * J + j + 1)
                act.activation(xThi[par][:, :, j * P:(j + 1) * P],
                               ps_t[j % 2][:, :].rearrange("p (c n) -> p c n", c=KD), ACT.Copy)\
                   .then_inc(xThi_ready, 1)

            for kind in ("regroup", "high_up", "turn_high", "high_dn", "turn_low", "back", "low_dn"):
                for i in range(sum(a == kind for a, _, _ in FOLD)):
                    fold_step(kind, i)
                    if kind == "back" and i % 4 == 3:
                        keep_xT_hi(0, 0, i // 4)
                if kind == "high_up":
                    act.wait_ge(bcol_turned, 1)
                    act.activation(bcol, ps[3][:, 256:256 + 2 * KH], ACT.Copy).then_inc(bcol_kept, 1)
                if kind == "turn_high":
                    act.wait_ge(bias_low, 1)
                    act.activation(yb, ps[3][:, 256:256 + KH], ACT.Copy).then_inc(yb_kept, 1)
            act.wait_ge(gelu_bias_ready, 1)

            def body(t, par, first, last):
                for k in range(KH):
                    if k == 0 and not last:
                        square(t + 1)
                    s = t * KH + k
                    act.wait_ge(h_ready, s + 1)
                    wait(act, glo_ready, s - 1)
                    act.activation(g32[:, k % 2, :], ps_h[k % 2][:, :], ACT.Gelu, bias=gelu_bias[:, k:k + 1])\
                       .then_inc(gelu_ready, 1)
                    if not last and 10 <= k < 10 + J:
                        keep_xT_hi(t + 1, 1 - par, k - 10)

            steps(act, body)

        @block.vector
        def _(dve):
            nc.vector.memset(decay[:, :], DECAY).then_inc(const_base, 1)
            nc.vector.memset(keep[:, :], -1).then_inc(const_base, 1)
            nc.vector.memset(carry[:, :], 0.0).then_inc(carry_saved, 1)
            dve.wait_ge(const_base, 2)
            nc.vector.memset(decay[:, :].rearrange("p (b i) -> p b i", i=Q)[:, :, 0:1], 0.0).then_inc(const_ready, 1)
            nc.vector.memset(keep[:, STEPS_PER_BATCH - 1:T:STEPS_PER_BATCH], 0).then_inc(const_ready, 1)

            dve.wait_ge(ident_ready, 1)
            nc.vector.reduce_sum(same_e, ident[:, :].rearrange("p (e k) -> p e k", e=E), axis=mybir.AxisListType.X)\
                .then_inc(mask_ready, 1)

            def path_products(dn, first, stages, places, full, spare, outer):
                prev = None
                for stage in range(stages):
                    n = outer << (stage + 1)
                    cur = (full if (stages - 1 - stage) % 2 == 0 else spare)[:, 0:n]
                    bank, col = places[stage]
                    dve.wait_ge(coef_spread, spreads(dn, first + max(stage, 3)))
                    if prev is None:
                        last = nc.vector.tensor_copy(cur, ps[bank][:, col:col + n])
                    else:
                        dve.wait_ge(path_product, spreads(dn, first + stage - 1))
                        banks = max(1, n // 512)
                        m = n // banks
                        for c in range(banks):
                            coef = ps[bank + c][:, col:col + m].rearrange("p (o a l) -> p o a l", o=outer // banks, a=2)
                            last = path_stage(nc.vector, cur[:, c * m:(c + 1) * m],
                                              prev[:, c * m // 2:(c + 1) * m // 2], coef, stage)
                    last.then_inc(path_product, 1)
                    prev = cur

            def low_products(dn):
                if dn:
                    dve.wait_ge(low_matrix_ready, 1)
                path_products(dn, 0, LOWS, LOW_PLACE, half[:, :], flat(LX[:, dn, :, :]), KH)

            def high_products(dn):
                if dn:
                    dve.wait_ge(high_matrix_ready, 1)
                path_products(dn, LOWS, HIGH, HIGH_PLACE, high_full, high_half, R)

            def fold_step(kind, i):
                n = fold_at(kind, i)
                bank = ps_f[n % 3]
                if FOLD[n][2] == "dve":
                    dve.wait_ge(fold_made, n + 1)
                    nc.vector.tensor_copy(*kept(kind, i, bank)).then_inc(fold_kept["dve"], 1)
                elif kind == "high_up":
                    dve.wait_ge(hi_split, i + 1)
                    nc.vector.tensor_tensor(out=w1_columns(W1lo, i), in0=columns(bank),
                                            in1=w1_columns(W1hi, i).bitcast(f32), op=ALU.subtract)\
                        .then_inc(fold_kept["dve"], 1)
                elif kind == "low_dn":
                    dve.wait_ge(hi_split, R + i + 1)
                    nc.vector.tensor_tensor(out=W2lo[:, i, :], in0=bank[:, :], in1=W2hi[:, i, :].bitcast(f32),
                                            op=ALU.subtract).then_inc(fold_kept["dve"], 1)

            def scan_chunk(u, j):
                n = u * J + j
                if j == 0:
                    dve.wait_ge(squared, u + 1)
                wait(dve, gate_turned, n)
                nc.vector.transpose(kvT[:, :, :].rearrange("p b i -> p (b i)"), kv[:, j, :]).then_inc(kv_turned, 1)
                dve.wait_ge(kv_turned, n + 1)
                dve.wait_ge(carry_saved, n + 1)
                nc.vector.scalar_tensor_tensor(out=kvT[:, :, 0], in0=carry[:, :], scalar=DECAY, in1=kvT[:, :, 0],
                                               op0=ALU.mult, op1=ALU.add).then_inc(carry_added, 1)
                dve.wait_ge(carry_added, n + 1)
                flat = kvT[:, :, :].rearrange("p b i -> p (b i)")
                nc.vector.tensor_tensor_scan(out=flat, data0=decay[:, :], data1=flat, initial=0.0,
                                             op0=ALU.mult, op1=ALU.add).then_inc(scanned, 1)
                dve.wait_ge(scanned, n + 1)
                if j < J - 1:
                    nc.vector.tensor_copy(carry[:, :], kvT[:, :, Q - 1]).then_inc(carry_saved, 1)
                else:
                    nc.vector.tensor_scalar(carry[:, :].bitcast(i32), kvT[:, :, Q - 1].bitcast(i32),
                                            keep[:, bass.ds(u, 1)], None, ALU.bitwise_and).then_inc(carry_saved, 1)
                nc.vector.transpose(kv[:, j, :], flat).then_inc(gate_turned, 1)

            def stats1(u, x):
                dve.wait_ge(x_loaded, (u + 1) * (G * NX))
                for j in range(J):
                    nc.vector.bn_stats(st1[:, j, :], x[:, j, :]).then_inc(stats1_done, 1)
                dve.wait_ge(stats1_done, u * J + J)
                nc.vector.memset(wait_pad[:, J:J + 1], 0.0)
                for j in range(J):
                    nc.vector.bn_aggr(mv1[:, j, :], st1[:, j, :]).then_inc(mean1_ready, 1)

            def gate(u, x, j):
                n = u * J + j
                if j == 0:
                    dve.wait_ge(rstd1_ready, u + 1)
                    dve.wait_ge(gate_turned, u * J + J)
                    dve.wait_ge(mean1_ready, u * J + J)
                nc.vector.scalar_tensor_tensor(out=kv[:, j, :], in0=x[:, j, :], scalar=mv1[:, j, 0:1], in1=kv[:, j, :],
                                               op0=ALU.subtract, op1=ALU.mult).then_inc(gated, 1)
                dve.wait_ge(gated, n + 1)
                nc.vector.scalar_tensor_tensor(out=x[:, j, :], in0=kv[:, j, :], scalar=rstd1[:, j:j + 1],
                                               in1=x[:, j, :], op0=ALU.mult, op1=ALU.add).then_inc(x1_ready, 1)
                dve.wait_ge(x1_ready, n + 1)
                nc.vector.bn_stats(st2[:, j, :], x[:, j, :]).then_inc(stats2_done, 1)
                dve.wait_ge(stats2_done, n + 1)
                nc.vector.memset(wait_pad[:, j:j + 1], 0.0)
                nc.vector.bn_aggr(mv2[:, j, :], st2[:, j, :]).then_inc(mean2_ready, 1)

            def normalise(u, x, j):
                n = u * J + j
                dve.wait_ge(rstd2_ready, n + 1)
                dve.wait_ge(mean2_ready, n + 1)
                nc.vector.tensor_scalar(kv[:, j, :], x[:, j, :], mv2[:, j, 0:1], rstd2[:, j:j + 1],
                                        ALU.subtract, ALU.mult).then_inc(xn_ready, 1)
                dve.wait_ge(xn_ready, n + 1)
                nc.vector.tensor_tensor(out=x[:, j, :], in0=x[:, j, :], in1=bias_row[:, :], op=ALU.add)\
                    .then_inc(bias_added, 1)

            def keep_xT_lo(u, par, j):
                dve.wait_ge(xThi_ready, u * J + j + 1)
                hi = xThi[par][:, :, j * P:(j + 1) * P].bitcast(f32)
                nc.vector.tensor_tensor(out=xTlo[par][:, :, j * P:(j + 1) * P],
                                        in0=ps_t[j % 2][:, :].rearrange("p (c n) -> p c n", c=KD), in1=hi,
                                        op=ALU.subtract).then_inc(xTlo_ready, 1)

            low_products(0)
            high_products(0)
            dve.wait_ge(path_product, LOWS)
            dve.wait_ge(top_loaded[0], NX)
            top_stage(nc.vector, 0).then_inc(low_matrix_ready, 1)
            dve.wait_ge(const_ready, 2)
            dve.wait_ge(bias_loaded, 4 * NX)
            nc.vector.tensor_tensor(out=bias_row[:, :], in0=bias_row[:, :], in1=bias_tmp, op=ALU.add)\
                .then_inc(bias_row_ready, 1)
            dve.wait_ge(bias_row_ready, 1)
            for j in range(J):
                scan_chunk(0, j)
            stats1(0, xs[0])
            for j in range(J):
                gate(0, xs[0], j)
            for j in range(J):
                normalise(0, xs[0], j)
            low_products(1)
            high_products(1)
            for kind in ("regroup", "high_up", "turn_high", "high_dn", "turn_low", "back", "low_dn"):
                for i in range(sum(a == kind for a, _, _ in FOLD)):
                    fold_step(kind, i)
                    if kind == "back" and i % 4 == 3:
                        keep_xT_lo(0, 0, i // 4)

            def finish(t, par, j):
                nc.vector.tensor_tensor(out=xs[par][:, j, :], in0=ps_y[j][:, :], in1=xs[par][:, j, :], op=ALU.add)\
                    .then_inc(out_ready, 1)

            def finish_step(t, par):
                dve.wait_ge(y_part, (t + 1) * KH)
                dve.wait_ge(bias_added, (t + 1) * J)
                for j in range(J):
                    finish(t, par, j)

            def body(t, par, first, last):
                nxt = xs[1 - par]
                for k in range(KH):
                    s = t * KH + k
                    slot = k % 2
                    dve.wait_ge(gelu_ready, s + 1)
                    wait(dve, y_part, s - 1)
                    nc.vector.tensor_copy(ghi[:, slot, :], g32[:, slot, :]).then_inc(ghi_ready, 1)
                    dve.wait_ge(ghi_ready, s + 1)
                    nc.vector.tensor_tensor(out=glo[:, slot, :], in0=g32[:, slot, :],
                                            in1=ghi[:, slot, :].bitcast(f32), op=ALU.subtract).then_inc(glo_ready, 1)
                    if k == LAG - 1 and not first:
                        finish_step(t - 1, 1 - par)
                    if last:
                        continue
                    u = t + 1
                    if 2 <= k < 2 + J:
                        scan_chunk(u, k - 2)
                    if k == 6:
                        stats1(u, nxt)
                    if 7 <= k < 7 + J:
                        gate(u, nxt, k - 7)
                    if 8 <= k < 8 + J:
                        normalise(u, nxt, k - 8)
                    if 10 <= k < 10 + J:
                        keep_xT_lo(u, 1 - par, k - 10)

            steps(dve, body)
            finish_step(T - 1, (T - 1) % 2)

        @block.tensor
        def _(pe):
            pe.wait_ge(ident_ready, 1)
            pe.wait_ge(sel_ready, 2 * LOW)

            def spread(dn):
                def stage_spread(src, place, stage, order):
                    rows, off, n_src = src_place(stage)
                    bank, col = place
                    n = KH << (stage + 1)
                    kb = max(1, n // 512)
                    kn = KH // kb
                    v = src[0:rows, off:off + n_src].rearrange(order, o=KH, a=2, b=2)
                    for c in range(kb):
                        for bit in range(2):
                            last = nc.tensor.matmul(ps[bank + c][:, col:col + n // kb], sel[0:rows, stage, bit, :],
                                                    v[:, c * kn:(c + 1) * kn, :, :, bit],
                                                    start=(bit == 0), stop=(bit == 1))
                    last.then_inc(coef_spread, 1)

                def low():
                    pe.wait_ge(low_loaded[dn], LOWS * NX)
                    for stage in range(LOWS):
                        stage_spread(low_src[dn], LOW_PLACE[stage], stage, "q (o l a b) -> q o a l b")

                def high():
                    pe.wait_ge(high_loaded[dn], HIGH_LOADS * NX)
                    if dn:
                        pe.wait_ge(path_product, UP_DONE)
                    for b in range(HIGH):
                        stage_spread(high_src[dn], HIGH_PLACE[b], b, "q (l o a b) -> q o a l b")

                return low, high

            def fold_step(kind, i):
                n = fold_at(kind, i)
                bank = ps_f[n % 3]
                if n >= 3:
                    who, count = kept_count[n - 3]
                    pe.wait_ge(fold_kept[who], count)
                if kind == "low_dn":
                    wait_kept(pe, "back", i)
                    nc.tensor.matmul(bank[:, :], LX[:, 1, i, :], wcon[:, i, :], start=True, stop=True)\
                        .then_inc(fold_made, 1)
                    return
                for c in range(4):
                    o = bank[:, c * P:(c + 1) * P]
                    block_c = slice(c * P, (c + 1) * P)
                    if kind == "WT":
                        last = nc.tensor.transpose(o, wexp[:, c, i * P:(i + 1) * P], ident[:, :])
                    elif kind == "low_up":
                        last = nc.tensor.matmul(o, WT[:, i, block_c], LX[:, 0, i, :], start=True, stop=True)
                    elif kind == "regroup":
                        last = nc.tensor.transpose(o, wexp[:, c, i * P:(i + 1) * P], ident[:, :])
                    elif kind == "high_up":
                        last = nc.tensor.matmul(o, Z[:, i, block_c], HX[:, 0, i, :], start=True, stop=True)
                    elif kind == "turn_high":
                        last = nc.tensor.transpose(o, HX[:, 1, 4 * i + c, :], ident[:, :])
                    elif kind == "high_dn":
                        last = nc.tensor.matmul(o, wcon[:, i, block_c], HX[:, 1, i, :], start=True, stop=True)
                    elif kind == "turn_low":
                        last = nc.tensor.transpose(o, LX[:, 1, 4 * i + c, :], ident[:, :])
                    elif kind == "back":
                        last = nc.tensor.transpose(o, Zd[:, c, i * P:(i + 1) * P], ident[:, :])
                last.then_inc(fold_made, 1)

            def turn_x(u, j):
                n = u * J + j
                pe.wait_ge(xn_ready, n + 1)
                wait(pe, xTlo_ready, n - 1)
                for c in range(KD):
                    last = nc.tensor.transpose(ps_t[j % 2][:, c * P:(c + 1) * P], kv[:, j, c * P:(c + 1) * P],
                                               ident[:, :])
                last.then_inc(xT_turned, 1)

            spread_low, spread_high = spread(0)
            spread_low()
            spread_high()
            for k in range(KH):
                if k % 4 == 0:
                    pe.wait_ge(wexp_loaded[k // 4], NX)
                fold_step("WT", k)
            pe.wait_ge(low_matrix_ready, 1)
            for k in range(KH):
                wait_kept(pe, "WT", k)
                fold_step("low_up", k)
            spread_low, spread_high = spread(1)
            spread_low()
            spread_high()
            wait_kept(pe, "low_up", KH - 1)
            for r in range(R):
                fold_step("regroup", r)
            pe.wait_ge(high_matrix_ready, 1)
            for r in range(R):
                wait_kept(pe, "regroup", r)
                fold_step("high_up", r)
            pe.wait_ge(path_product, spreads(1, LOW - 2))
            pe.wait_ge(bias_loaded, 4 * NX)
            nc.tensor.transpose(ps[3][:, 256:256 + 2 * KH], bias_rows, ident[0:2 * KH, 0:2 * KH]).then_inc(bcol_turned, 1)
            pe.wait_ge(high_matrix_ready, 2)
            for q in range(R // 4):
                fold_step("turn_high", q)
            pe.wait_ge(bcol_kept, 1)
            for k in range(KH):
                last = nc.tensor.matmul(ps[3][:, 256 + k:257 + k], LX[:, 0, k, :], bcol[:, k:k + 1], start=True, stop=True)
            last.then_inc(bias_low, 1)
            for r in range(R):
                if r % (R // 2) == 0:
                    pe.wait_ge(wcon_loaded[r // (R // 2)], E * NX)
                wait_kept(pe, "turn_high", r // 4)
                fold_step("high_dn", r)
            pe.wait_ge(low_matrix_ready, 2)
            for q in range(KH // 4):
                fold_step("turn_low", q)
            wait_kept(pe, "high_dn", R - 2)
            wait_kept(pe, "high_dn", R - 1)
            pe.wait_ge(yb_kept, 1)
            for k in range(KH):
                fold_step("back", k)
                if k % 4 == 3:
                    turn_x(0, k // 4)
            wait_kept(pe, "turn_low", KH // 4 - 2)
            wait_kept(pe, "turn_low", KH // 4 - 1)
            for k in range(KH):
                fold_step("low_dn", k)

            def up_product(t, par, k):
                if k == 0:
                    pe.wait_ge(xTlo_ready, (t + 1) * J)
                wait(pe, gelu_ready, t * KH + (k - 1))
                terms = [(w, v) for c in range(KD) for w, v in
                         ((W1hi[:, k, c, :], xThi[par][:, c, :]), (W1hi[:, k, c, :], xTlo[par][:, c, :]),
                          (W1lo[:, k, c, :], xThi[par][:, c, :]))]
                for i, (w, v) in enumerate(terms):
                    last = nc.tensor.matmul(ps_h[k % 2][:, :], w, v, start=(i == 0), stop=(i == len(terms) - 1))
                last.then_inc(h_ready, 1)

            def down_product(t, k, first):
                s = t * KH + k
                pe.wait_ge(glo_ready, s + 1)
                for j in range(J):
                    if k == 0 and not first:
                        pe.wait_ge(out_ready, (t - 1) * J + (j + 1))
                    tok = slice(j * P, (j + 1) * P)
                    for i, (g, w) in enumerate(((ghi, W2hi), (ghi, W2lo), (glo, W2hi))):
                        last = nc.tensor.matmul(ps_y[j][:, :], g[:, k % 2, tok], w[:, k, :],
                                                start=(k == 0 and i == 0), stop=(k == KH - 1 and i == 2))
                last.then_inc(y_part, 1)

            def body(t, par, first, last):
                for k in range(KH):
                    up_product(t, par, k)
                    if k >= LAG:
                        down_product(t, k - LAG, first)
                    elif not first:
                        down_product(t - 1, k - LAG + KH, False)
                    if not last and 9 <= k < 9 + J:
                        turn_x(t + 1, k - 9)

            steps(pe, body)
            for k in range(KH - LAG, KH):
                down_product(T - 1, k, False)


_INS = ['x', 'ctx_1024', 'L0_ffn_W_exp', 'L0_ffn_b_exp', 'L0_ffn_up_weights', 'L0_ffn_up_bias',
        'L0_ffn_down_weights', 'L0_ffn_W_con', 'L0_ffn_b_con', 'L0_ffn_down_bias']


def kernel(**inputs):
    import numpy as _np
    import concourse.bacc as _bacc
    from concourse import mybir as _mybir
    from concourse.bass_utils import run_bass_kernel_spmd as _run

    nc = _bacc.Bacc("TRN2", target_bir_lowering=False, num_devices=1)
    arrays, args = {}, []
    for name in _INS:
        a = _np.ascontiguousarray(inputs[name])
        arrays[f"in_{name}_dram"] = a
        args.append(nc.dram_tensor(f"in_{name}_dram", a.shape, _mybir.dt.from_np(a.dtype), kind="ExternalInput").ap())
    shape = inputs['x'].shape
    args.append(nc.dram_tensor("out_dram", shape, _mybir.dt.float32, kind="ExternalOutput").ap())
    xattn_ffn_program(nc, *args)
    r = _run(nc, [arrays], core_ids=[0])
    return r.results[0]["out_dram"]
```

```python
import concourse.bass as bass
from concourse import mybir
from contextlib import ExitStack


def xattn_ffn_program(nc, x_in, ctx_in, w_exp, b_exp, up_w, up_bias, down_w, w_con, b_con, down_bias, out):
    f32 = mybir.dt.float32
    f32r = mybir.dt.float32r
    i32 = mybir.dt.int32
    ALU = mybir.AluOpType
    ACT = mybir.ActivationFunctionType

    P = 128
    B, S, D = x_in.shape
    H = w_exp.shape[1]
    KD = D // P
    KH = H // P
    LOW = 7
    HIGH = up_w.shape[0] - LOW
    PAIRS = KH // 2
    E = P // KH
    R = P // E
    G = 4
    Q = 32
    J = 4
    T = B * S // (J * P)
    STEPS_PER_BATCH = S // (Q * J)
    DECAY = 0.9
    EPS = 1e-5
    LAG = 2
    KEEP_AT = (KH - 3, KH - 2)
    NX = 16
    MOVES = G * G

    def token_rows(a):
        return a.rearrange("b s d -> (b s) d").rearrange("(g t j i) d -> g t i j d", g=G, t=T, j=J, i=Q)

    x_rows, ctx_rows, out_rows = token_rows(x_in), token_rows(ctx_in), token_rows(out)

    es = ExitStack()
    with es:
        def sb(name, shape, dt=f32, stack=es):
            return stack.enter_context(nc.sbuf_tensor(name, shape, dt))

        def sem(name):
            return es.enter_context(nc.semaphore(name))

        fold = ExitStack()
        wexp = sb("wexp", [P, KD, H], stack=fold)
        WT = sb("WT", [P, KH, D], stack=fold)
        wcon = sb("wcon", [P, KH, D], stack=fold)
        Z = sb("Z", [P, KH, D], stack=fold)
        HX = sb("HX", [P, 2, R, P], stack=fold)
        LX = sb("LX", [P, 2, KH, P], stack=fold)
        half = sb("half", [P, KH * P // 2], stack=fold)
        sel = sb("sel", [P, LOW - 1, 2, P], stack=fold)
        fold.close()
        W1hi = sb("W1hi", [P, KH, KD, P], f32r)
        W1lo = sb("W1lo", [P, KH, KD, P], f32r)
        W2hi = sb("W2hi", [P, KH, D], f32r)
        W2lo = sb("W2lo", [P, KH, D], f32r)
        xThi, xTlo = [], []
        for par in range(2):
            xThi.append(sb(f"xThi{par}", [P, KD, J * P], f32r))
            xTlo.append(sb(f"xTlo{par}", [P, KD, J * P], f32r))
        g32 = sb("g32", [P, 2, J * P])
        ghi = sb("ghi", [P, 2, J * P], f32r)
        glo = sb("glo", [P, 2, J * P], f32r)
        xs = [sb(f"x{par}", [P, J, D]) for par in range(2)]
        kv = sb("kv", [P, J, D])
        kvT = sb("kvT", [P, D // Q, Q])
        decay = sb("decay", [P, D])
        bias_row = sb("bias_row", [P, D])
        ident = sb("ident", [P, P])
        carry = sb("carry", [P, D // Q])
        keep = sb("keep", [P, T + 1], i32)
        st1 = sb("st1", [P, J, 6])
        mv1 = sb("mv1", [P, J, 2])
        ve1 = sb("ve1", [P, J])
        rstd1 = sb("rstd1", [P, J])
        st2 = sb("st2", [P, J, 6])
        mv2 = sb("mv2", [P, J, 2])
        ve2 = sb("ve2", [P, J])
        rstd2 = sb("rstd2", [P, J])
        neg_half = sb("neg_half", [P, J])
        wait_pad = sb("wait_pad", [P, J + 1])
        eps = sb("eps", [P, J])
        gelu_bias = sb("gelu_bias", [P, KH])
        flat1 = xs[1][:, :, :].rearrange("p j d -> p (j d)")
        hc_up = flat1[:, 0:HIGH * PAIRS * 4].rearrange("p (s m e) -> p s m e", s=HIGH, m=PAIRS)
        same_e = flat1[:, 128:128 + E]
        bias_rows = flat1[0:2 * KH, 256:256 + P]
        bcol = flat1[:, 384:384 + 2 * KH]
        yb = flat1[:, 448:448 + KH]
        ybt = flat1[:, 512:512 + 4 * PAIRS].rearrange("p (e m) -> p e m", e=4)
        high_half = flat1[:, 640:640 + R * KH // 2]
        high_full = flat1[:, 768:768 + R * KH]
        bias_tmp = flat1[:, 1024:1024 + D]

        def flat(a):
            return a.rearrange("p a b -> p (a b)")
        low_src = [flat(Z[:, 0:8, :]), flat(wcon[:, 0:8, :])]
        low_src_hi = [W1lo[:, 8:16, :, :].rearrange("p a b n -> p (a b n)"), flat(W2lo[:, 0:8, :])]
        low_src_lo = [flat(W2lo[:, 0:8, :]), flat(W2hi[:, 0:8, :])]
        sel_r = [a[:, 0:4 * P].rearrange("p (s b n) -> p s b n", s=2, b=2) for a in low_src_hi]
        top_src = [flat(Z[:, 8:16, :]), flat(wcon[:, 8:16, :])]
        high_src = [flat(HX[:, 1, 0:8, :]), flat(HX[:, 1, 8:16, :])]

        ps = [es.enter_context(nc.psum_tensor(f"ps{i}", [P, 512], f32)) for i in range(8)]
        ps_h, ps_y = ps[0:2], ps[4:8]
        ps_f = ps[5:8]

        low_loaded = [sem("low_up_loaded"), sem("low_dn_loaded")]
        top_loaded = [sem("top_up_loaded"), sem("top_dn_loaded")]
        coef_loaded = sem("coef_loaded")
        bias_loaded = sem("bias_loaded")
        wexp_loaded = [sem(f"wexp_loaded{c}") for c in range(4)]
        wcon_loaded = [sem("wcon_low_loaded"), sem("wcon_high_loaded")]
        x_loaded = sem("x_loaded")
        ctx_loaded = sem("ctx_loaded")
        out_stored = sem("out_stored")
        ident_zero = sem("ident_zero")
        ident_ready = sem("ident_ready")
        sel_zero = sem("sel_zero")
        sel_ready = sem("sel_ready")
        const_ready = sem("const_ready")
        const_base = sem("const_base")
        neg_ready = sem("neg_ready")
        mask_ready = sem("mask_ready")
        sel_rounded = sem("sel_rounded")
        coef_hi = sem("coef_hi")
        coef_lo = sem("coef_lo")
        coef_spread = sem("coef_spread")
        path_product = sem("path_product")
        low_matrix_ready = sem("low_matrix_ready")
        high_matrix_ready = sem("high_matrix_ready")
        bcol_turned = sem("bcol_turned")
        bcol_kept = sem("bcol_kept")
        bias_low = sem("bias_low")
        yb_kept = sem("yb_kept")
        yb_step = sem("yb_step")
        gelu_bias_ready = sem("gelu_bias_ready")
        fold_made = sem("fold_made")
        fold_kept = {"act": sem("fold_kept_act"), "dve": sem("fold_kept_dve")}
        hi_split = sem("hi_split")
        bias_row_ready = sem("bias_row_ready")
        high_loaded = [sem("high_up_loaded"), sem("high_dn_loaded")]
        HIGH_LOADS = KH - 1

        squared = sem("squared")
        kv_turned = sem("kv_turned")
        carry_added = sem("carry_added")
        scanned = sem("scanned")
        carry_saved = sem("carry_saved")
        gate_turned = sem("gate_turned")
        stats1_done = sem("stats1_done")
        mean1_ready = sem("mean1_ready")
        eps1_added = sem("eps1_added")
        rstd1_ready = sem("rstd1_ready")
        gated = sem("gated")
        x1_ready = sem("x1_ready")
        stats2_done = sem("stats2_done")
        mean2_ready = sem("mean2_ready")
        eps2_added = sem("eps2_added")
        rstd2_ready = sem("rstd2_ready")
        xn_ready = sem("xn_ready")
        bias_added = sem("bias_added")
        xn_turned = sem("xn_turned")
        xT_moved = sem("xT_moved")
        xThi_ready = sem("xThi_ready")
        xTlo_ready = sem("xTlo_ready")
        h_ready = sem("h_ready")
        gelu_ready = sem("gelu_ready")
        ghi_ready = sem("ghi_ready")
        glo_ready = sem("glo_ready")
        y_part = sem("y_part")
        y_last = sem("y_last")
        out_ready = sem("out_ready")

        def xT_slots(u, par):
            if isinstance(u, int) and u == 0:
                return xTlo[0], xThi[0], xThi[0]
            return xThi[par], xTlo[par], xTlo[par]

        def wait(eng, semaphore, value):
            if isinstance(value, int) and value <= 0:
                return
            eng.wait_ge(semaphore, value)

        block = es.enter_context(nc.Block())

        def steps(eng, body):
            body(0, 0, first=True, last=False)
            with eng.Fori(1, T - 1, 2) as t:
                body(t, 1, first=False, last=False)
                body(t + 1, 0, first=False, last=False)
            body(T - 1, (T - 1) % 2, first=False, last=True)

        FOLD = [("WT", k, "dve" if k % 2 and k < KH // 4 else "act") for k in range(KH)]
        FOLD += [("low_up", k, "act") for k in range(KH)]
        FOLD += [("regroup", r, "act") for r in range(R)]
        FOLD += [("high_up", r, "split") for r in range(R)]
        FOLD += [("turn_high", q, "act") for q in range(R // 4)]
        FOLD += [("high_dn", r, "act") for r in range(R)]
        FOLD += [("turn_low", q, ("act", "dve")[q % 2]) for q in range(KH // 4)]
        FOLD += [("back", k, ("act", "dve")[k % 2]) for k in range(KH)]
        FOLD += [("low_dn", k, "split") for k in range(KH)]

        kept_count, kept_so_far = [], {"act": 0, "dve": 0}
        for _, _, who in FOLD:
            who = "dve" if who == "split" else who
            kept_so_far[who] += 1
            kept_count.append((who, kept_so_far[who]))

        def wait_kept(eng, kind, i):
            who, count = kept_count[fold_at(kind, i)]
            eng.wait_ge(fold_kept[who], count)

        def fold_at(kind, i):
            return [(a, b) for a, b, _ in FOLD].index((kind, i))

        def src_place(stage):
            n = 4 * KH << stage
            return (P // 2) >> stage, n - 4 * KH, n

        LOW_PLACE = [(0, 448), (0, 384), (0, 256), (0, 0), (1, 0), (2, 0)]
        HIGH_PLACE = [(4, 448), (4, 384), (4, 256), (4, 0)]
        LOWS = LOW - 1
        PARTED = range(LOWS - 2, LOWS)
        def spreads(dn, stage):
            return dn * (LOWS + HIGH) + stage + 1
        UP_DONE = LOWS + HIGH
        ALL_DONE = 2 * UP_DONE

        def path_stage(eng, cur, prev, coef, stage):
            lanes, outer = coef.shape[0], coef.shape[1]
            return eng.tensor_tensor(out=cur.rearrange("p (o a l) -> p o a l", o=outer, a=2),
                                     in0=prev.rearrange("p (o l) -> p o l", o=outer).unsqueeze(2)
                                     .to_broadcast([lanes, outer, 2, 1 << stage]), in1=coef, op=ALU.mult)

        def top_stage(eng, dn):
            src = top_src[dn].rearrange("p (o l a b) -> p o a l b", o=KH, a=2, b=2)
            for bit in range(2):
                lanes = slice(bit * P // 2, (bit + 1) * P // 2)
                last = path_stage(eng, flat(LX[:, dn, :, :])[lanes], half[lanes], src[lanes, :, :, :, bit], LOW - 1)
            return last

        def columns(bank):
            return bank[:, :].rearrange("p (c e k) -> p c e k", c=KD, e=E)

        def w1_columns(w, r):
            return w[:, :, :, r:P:R].rearrange("p k c e -> p c e k")

        def spread_columns(a, r):
            return a[:, :, r:H:R].rearrange("p c (k e) -> p c e k", e=E)

        Zd = Z[:, :, :].rearrange("p a b -> p (a b)").rearrange("p (c h) -> p c h", c=KD)

        def kept(kind, i, bank):
            whole = bank[:, :]
            if kind == "WT":
                return WT[:, i, :], whole
            if kind == "low_up":
                return wexp[:, :, i:H:KH].rearrange("p c (r e) -> p c e r", e=E),\
                    whole.rearrange("p (c e r) -> p c e r", c=KD, e=E)
            if kind == "regroup":
                return Z[:, i, :], whole
            if kind == "turn_high":
                return HX[:, 1, 4 * i:4 * i + 4, :].rearrange("p a b -> p (a b)"), whole
            if kind == "high_dn":
                return spread_columns(Zd, i), columns(bank)
            if kind == "turn_low":
                return LX[:, 1, 4 * i:4 * i + 4, :].rearrange("p a b -> p (a b)"), whole
            assert kind == "back"
            return wcon[:, i, :], whole

        @block.sync
        def _(sp):
            def load_tokens(dst, rows, t, loaded):
                for g in range(G):
                    sp.dma_start(dst[Q * g:Q * g + Q, :, :], rows[g, t]).then_inc(loaded, NX)

            def load_coefs(weights, dn):
                for stage in range(LOWS):
                    rows, off, n = src_place(stage)
                    src = weights[stage].rearrange("(k q l) a b -> q k (l a b)", k=KH, q=rows)
                    sp.dma_start(low_src[dn][0:rows, off:off + n].rearrange("q (k n) -> q k n", k=KH), src)\
                      .then_inc(low_loaded[dn], NX)

            def load_top(weights, dn):
                sp.dma_start(top_src[dn], weights[LOW - 1].rearrange("m a b -> (m a b)").partition_broadcast(P))\
                  .then_inc(top_loaded[dn], NX)

            def load_high(weights, dn):
                for b in range(HIGH):
                    rows, off, n = src_place(b)
                    top = KH >> (b + 1)
                    src = weights[LOW + b].rearrange("(i l e n) x y -> i e l (n x y)", i=top, e=E, n=R)
                    dst = high_src[dn][0:rows, off:off + n].rearrange("q (l n) -> q l n", l=1 << b)
                    for i in range(top):
                        sp.dma_start(dst[i:rows:top], src[i]).then_inc(high_loaded[dn], NX)

            wexp_src = w_exp.rearrange("(c p) h -> p c h", p=P)

            def load_wexp(q):
                part = slice(q * H // 4, (q + 1) * H // 4)
                sp.dma_start(wexp[:, :, part], wexp_src[:, :, part]).then_inc(wexp_loaded[q], NX)

            load_wexp(0)
            load_coefs(up_w, 0)
            for q in range(1, 4):
                load_wexp(q)
            load_top(up_w, 0)
            load_high(up_w, 0)
            load_coefs(down_w, 1)
            load_tokens(kv, ctx_rows, 0, ctx_loaded)
            load_tokens(xs[0], x_rows, 0, x_loaded)
            load_top(down_w, 1)
            load_high(down_w, 1)
            wcon_src = w_con.rearrange("(k e r) d -> e k (r d)", e=E, r=R)
            for part in range(2):
                if part == 0:
                    sp.wait_ge(coef_spread, spreads(1, LOWS - 1))
                else:
                    sp.wait_ge(low_matrix_ready, 2)
                cols = slice(part * R * D // 2, (part + 1) * R * D // 2)
                for e in range(E):
                    sp.dma_start(flat(wcon[KH * e:KH * (e + 1), :, :])[:, cols], wcon_src[e][:, cols])\
                      .then_inc(wcon_loaded[part], NX)

            turned = kv[:, :, :].rearrange("p j d -> p (j d)").rearrange("p (c q n) -> p c q n", q=G, n=P)

            def move_xT(u, par):
                whole = xT_slots(u, par)[2]
                sp.wait_ge(xn_turned, (u + 1) * J)
                for q in range(G):
                    for g in range(G):
                        sp.dma_start(whole[Q * q:Q * q + Q, :, g * P:(g + 1) * P].bitcast(f32),
                                     turned[Q * g:Q * g + Q, :, q, :]).then_inc(xT_moved, NX)

            sp.wait_ge(fold_made, fold_at("high_up", R - 1) + 1)
            move_xT(0, 0)
            sp.wait_ge(xT_moved, MOVES * NX)
            load_tokens(kv, ctx_rows, 1, ctx_loaded)

            def body(t, par, first, last):
                if first:
                    sp.wait_ge(high_matrix_ready, 2)
                    sp.wait_ge(bias_row_ready, 1)
                    sp.wait_ge(gelu_bias_ready, 1)
                else:
                    sp.wait_ge(out_ready, t * J)
                    for g in range(G):
                        sp.dma_start(out_rows[g, t - 1], xs[1 - par][Q * g:Q * g + Q, :, :])\
                          .then_inc(out_stored, NX)
                if not last:
                    if not first:
                        sp.wait_ge(out_stored, t * (G * NX))
                    load_tokens(xs[1 - par], x_rows, t + 1, x_loaded)
                    move_xT(t + 1, 1 - par)

            def next_ctx(t):
                sp.wait_ge(xT_moved, (t + 2) * (MOVES * NX))
                load_tokens(kv, ctx_rows, t + 2, ctx_loaded)

            body(0, 0, True, False)
            next_ctx(0)
            with sp.Fori(1, T - 3, 2) as t:
                body(t, 1, False, False)
                next_ctx(t)
                body(t + 1, 0, False, False)
                next_ctx(t + 1)
            body(T - 3, (T - 3) % 2, False, False)
            next_ctx(T - 3)
            body(T - 2, (T - 2) % 2, False, False)
            body(T - 1, (T - 1) % 2, False, True)
            for h in range(2):
                sp.wait_ge(out_ready, (T - 1) * J + (h + 1) * J // 2)
                chunks = slice(h * J // 2, (h + 1) * J // 2)
                for g in range(G):
                    sp.dma_start(out_rows[g, T - 1, :, chunks], xs[(T - 1) % 2][Q * g:Q * g + Q, chunks, :])\
                      .then_inc(out_stored, NX)
            sp.wait_ge(out_stored, (T + 1) * G * NX)

        @block.gpsimd
        def _(pool):
            nc.gpsimd.memset(ident[:, :], 0.0).then_inc(ident_zero, 1)
            pool.wait_ge(ident_zero, 1)
            nc.gpsimd.affine_select(out=ident[:, :], in_=ident[:, :], compare_op=ALU.not_equal, fill=1.0, base=0,
                                    pattern=[[-1, P]], channel_multiplier=1).then_inc(ident_ready, 1)
            pool.wait_ge(sel_zero, 1)
            for stage in range(LOWS):
                rows = (P // 2) >> stage
                for bit in range(2):
                    v = sel[0:rows, stage, bit, :].rearrange("q (a b) -> q a b", b=1 << stage)
                    nc.gpsimd.affine_select(out=v, in_=v, compare_op=ALU.not_equal, fill=1.0, base=bit,
                                            pattern=[[-1, P >> stage], [0, 1 << stage]], channel_multiplier=2)\
                        .then_inc(sel_ready, 1)
            nc.gpsimd.memset(neg_half[:, :], -0.5).then_inc(neg_ready, 1)
            nc.gpsimd.memset(eps[:, :], EPS).then_inc(neg_ready, 1)

            def high_matrix(dn):
                pool.wait_ge(path_product, ALL_DONE if dn else UP_DONE)
                pool.wait_ge(mask_ready, 1)
                if dn:
                    pool.wait_ge(coef_spread, ALL_DONE)
                nc.gpsimd.tensor_tensor(
                    out=HX[:, dn, :, :].rearrange("p r (e k) -> p r e k", e=E),
                    in0=high_full.rearrange("p (r k) -> p r k", r=R).unsqueeze(2).to_broadcast([P, R, E, KH]),
                    in1=same_e.unsqueeze(1).unsqueeze(3).to_broadcast([P, R, E, KH]), op=ALU.mult)\
                    .then_inc(high_matrix_ready, 1)

            def rstd(u):
                pool.wait_ge(mean1_ready, u * J + J)
                nc.gpsimd.tensor_tensor(out=ve1[:, :], in0=mv1[:, :, 1], in1=eps[:, :], op=ALU.add).then_inc(eps1_added, 1)
                pool.wait_ge(eps1_added, u + 1)
                nc.gpsimd.tensor_tensor(out=rstd1[:, :], in0=ve1[:, :], in1=neg_half[:, :], op=ALU.pow)\
                    .then_inc(rstd1_ready, 1)
                for j in range(J):
                    pool.wait_ge(mean2_ready, u * J + j + 1)
                    nc.gpsimd.tensor_tensor(out=ve2[:, j:j + 1], in0=mv2[:, j, 1:2], in1=eps[:, j:j + 1], op=ALU.add)\
                        .then_inc(eps2_added, 1)
                    pool.wait_ge(eps2_added, u * J + j + 1)
                    nc.gpsimd.tensor_tensor(out=rstd2[:, j:j + 1], in0=ve2[:, j:j + 1], in1=neg_half[:, j:j + 1],
                                            op=ALU.pow).then_inc(rstd2_ready, 1)

            high_matrix(0)
            pool.wait_ge(neg_ready, 2)
            pool.wait_ge(path_product, spreads(1, LOW - 2))
            pool.wait_ge(low_matrix_ready, 1)
            pool.wait_ge(top_loaded[1], NX)
            pool.wait_ge(high_matrix_ready, 1)
            top_stage(nc.gpsimd, 1).then_inc(low_matrix_ready, 1)
            pool.wait_ge(low_matrix_ready, 2)
            high_matrix(1)
            rstd(0)

            pool.wait_ge(coef_loaded, NX)
            pool.wait_ge(yb_kept, 1)
            n = 0

            def step(ins):
                nonlocal n
                n += 1
                ins.then_inc(yb_step, 1)

            for bit in range(HIGH):
                v = yb.rearrange("p (h s l) -> p h s l", s=2, l=1 << bit)
                c = hc_up[:, bit, :, :].rearrange("p (h l) e -> p h l e", l=1 << bit)
                tt = ybt.rearrange("p e (h l) -> p e h l", l=1 << bit)
                if n:
                    pool.wait_ge(yb_step, n)
                for e in range(4):
                    step(nc.gpsimd.tensor_tensor(out=tt[:, e], in0=v[:, :, e % 2, :], in1=c[:, :, :, e], op=ALU.mult))
                pool.wait_ge(yb_step, n)
                for o in range(2):
                    step(nc.gpsimd.tensor_tensor(out=v[:, :, o, :], in0=tt[:, 2 * o], in1=tt[:, 2 * o + 1], op=ALU.add))
            pool.wait_ge(yb_step, n)
            nc.gpsimd.tensor_tensor(out=gelu_bias[:, :], in0=yb, in1=bcol[:, KH:2 * KH], op=ALU.add)\
                .then_inc(gelu_bias_ready, 1)

            with pool.Fori(1, T) as u:
                rstd(u)

        @block.scalar
        def _(act):
            act.dma_start(bias_rows[0:KH, :], b_exp.rearrange("(k p) -> k p", p=P)).then_inc(bias_loaded, NX)
            act.dma_start(bias_rows[KH:2 * KH, :], up_bias.rearrange("(k p) -> k p", p=P)).then_inc(bias_loaded, NX)
            act.dma_start(hc_up, up_w[LOW:LOW + HIGH].rearrange("s (m p) a b -> p s m (a b)", p=P))\
               .then_inc(coef_loaded, NX)
            act.dma_start(bias_row[:, :], b_con.partition_broadcast(P)).then_inc(bias_loaded, NX)
            act.dma_start(bias_tmp, down_bias.partition_broadcast(P)).then_inc(bias_loaded, NX)

            def fold_step(kind, i):
                n = fold_at(kind, i)
                bank = ps_f[n % 3]
                act.wait_ge(fold_made, n + 1)
                if kind == "high_up":
                    act.activation(w1_columns(W1hi, i), columns(bank), ACT.Copy).then_inc(hi_split, 1)
                elif kind == "low_dn":
                    act.activation(W2hi[:, i, :], bank[:, :], ACT.Copy).then_inc(hi_split, 1)
                elif FOLD[n][2] == "act":
                    act.activation(*kept(kind, i, bank), ACT.Copy).then_inc(fold_kept["act"], 1)

            def square(u):
                act.wait_ge(ctx_loaded, (u + 1) * (G * NX))
                act.activation(kv[:, :, :], kv[:, :, :], ACT.Square).then_inc(squared, 1)

            def coefs_hi(dn):
                act.wait_ge(low_loaded[dn], LOWS * NX)
                if dn:
                    act.wait_ge(coef_spread, LOWS)
                for stage in PARTED:
                    rows, off, n = src_place(stage)
                    act.activation(low_src_hi[dn][0:rows, off:off + n], low_src[dn][0:rows, off:off + n], ACT.Copy)\
                       .then_inc(coef_hi, 1)

            for k in range(KH):
                if k == KH // 4:
                    coefs_hi(0)
                fold_step("WT", k)
            coefs_hi(1)
            square(0)
            for k in range(KH):
                fold_step("low_up", k)

            def keep_xT_hi(u, par, c):
                if c == 0:
                    act.wait_ge(xT_moved, (u + 1) * (MOVES * NX))
                hi, lo, whole = xT_slots(u, par)
                act.activation(hi[:, c, :], whole[:, c, :].bitcast(f32), ACT.Copy).then_inc(xThi_ready, 1)

            for kind in ("regroup", "high_up", "turn_high", "high_dn", "turn_low", "back", "low_dn"):
                for i in range(sum(a == kind for a, _, _ in FOLD)):
                    fold_step(kind, i)
                    if kind == "low_dn" and i % 4 == 1:
                        keep_xT_hi(0, 0, i // 4)
                if kind == "high_up":
                    act.wait_ge(bcol_turned, 1)
                    act.activation(bcol, ps[3][:, 256:256 + 2 * KH], ACT.Copy).then_inc(bcol_kept, 1)
                if kind == "turn_high":
                    act.wait_ge(bias_low, 1)
                    act.activation(yb, ps[3][:, 256:256 + KH], ACT.Copy).then_inc(yb_kept, 1)
            act.wait_ge(gelu_bias_ready, 1)

            def body(t, par, first, last):
                for k in range(KH):
                    if k == 0 and not last:
                        square(t + 1)
                    s = t * KH + k
                    act.wait_ge(h_ready, s + 1)
                    wait(act, glo_ready, s - 1)
                    act.activation(g32[:, k % 2, :].rearrange("p (j g i) -> p g j i", g=G, i=Q),
                                   ps_h[k % 2][:, :].rearrange("p (g j i) -> p g j i", g=G, i=Q),
                                   ACT.Gelu, bias=gelu_bias[:, k:k + 1]).then_inc(gelu_ready, 1)
                    if not last and k in KEEP_AT:
                        for c in range(KD // 2):
                            keep_xT_hi(t + 1, 1 - par, (k - KEEP_AT[0]) * 2 + c)

            steps(act, body)

        @block.vector
        def _(dve):
            nc.vector.memset(sel[:, :, :, :], 0.0).then_inc(sel_zero, 1)
            nc.vector.memset(decay[:, :], DECAY).then_inc(const_base, 1)
            nc.vector.memset(keep[:, :], -1).then_inc(const_base, 1)
            nc.vector.memset(carry[:, :], 0.0).then_inc(carry_saved, 1)
            dve.wait_ge(const_base, 2)
            nc.vector.memset(decay[:, :].rearrange("p (b i) -> p b i", i=Q)[:, :, 0:1], 0.0).then_inc(const_ready, 1)
            nc.vector.memset(keep[:, STEPS_PER_BATCH - 1:T:STEPS_PER_BATCH], 0).then_inc(const_ready, 1)

            dve.wait_ge(ident_ready, 1)
            nc.vector.reduce_sum(same_e, ident[:, :].rearrange("p (e k) -> p e k", e=E), axis=mybir.AxisListType.X)\
                .then_inc(mask_ready, 1)

            def path_products(dn, first, stages, places, full, spare, outer):
                prev = None
                for stage in range(stages):
                    n = outer << (stage + 1)
                    cur = (full if (stages - 1 - stage) % 2 == 0 else spare)[:, 0:n]
                    bank, col = places[stage]
                    dve.wait_ge(coef_spread, spreads(dn, first + max(stage, 3)))
                    if prev is None:
                        last = nc.vector.tensor_copy(cur, ps[bank][:, col:col + n])
                    else:
                        dve.wait_ge(path_product, spreads(dn, first + stage - 1))
                        banks = max(1, n // 512)
                        m = n // banks
                        for c in range(banks):
                            coef = ps[bank + c][:, col:col + m].rearrange("p (o a l) -> p o a l", o=outer // banks, a=2)
                            last = path_stage(nc.vector, cur[:, c * m:(c + 1) * m],
                                              prev[:, c * m // 2:(c + 1) * m // 2], coef, stage)
                    last.then_inc(path_product, 1)
                    prev = cur

            def coefs_lo(dn):
                if dn:
                    dve.wait_ge(coef_spread, LOWS)
                else:
                    dve.wait_ge(sel_ready, 2 * LOWS)
                rows = src_place(PARTED[0])[0]
                nc.vector.tensor_copy(sel_r[dn][0:rows], sel[0:rows, PARTED[0]:LOWS]).then_inc(sel_rounded, 1)
                for i, stage in enumerate(PARTED):
                    rows, off, n = src_place(stage)
                    v = low_src[dn][0:rows, off:off + n]
                    dve.wait_ge(coef_hi, dn * len(PARTED) + i + 1)
                    nc.vector.tensor_tensor(out=low_src_lo[dn][0:rows, off:off + n], in0=v,
                                            in1=low_src_hi[dn][0:rows, off:off + n].bitcast(f32), op=ALU.subtract)\
                        .then_inc(coef_lo, 1)

            def low_products(dn):
                if dn:
                    dve.wait_ge(low_matrix_ready, 1)
                path_products(dn, 0, LOWS, LOW_PLACE, half[:, :], flat(LX[:, dn, :, :]), KH)

            def high_products(dn):
                if dn:
                    dve.wait_ge(high_matrix_ready, 1)
                path_products(dn, LOWS, HIGH, HIGH_PLACE, high_full, high_half, R)

            def fold_step(kind, i):
                n = fold_at(kind, i)
                bank = ps_f[n % 3]
                if FOLD[n][2] == "dve":
                    dve.wait_ge(fold_made, n + 1)
                    nc.vector.tensor_copy(*kept(kind, i, bank)).then_inc(fold_kept["dve"], 1)
                elif kind == "high_up":
                    dve.wait_ge(hi_split, i + 1)
                    nc.vector.tensor_tensor(out=w1_columns(W1lo, i), in0=columns(bank),
                                            in1=w1_columns(W1hi, i).bitcast(f32), op=ALU.subtract)\
                        .then_inc(fold_kept["dve"], 1)
                elif kind == "low_dn":
                    dve.wait_ge(hi_split, R + i + 1)
                    nc.vector.tensor_tensor(out=W2lo[:, i, :], in0=bank[:, :], in1=W2hi[:, i, :].bitcast(f32),
                                            op=ALU.subtract).then_inc(fold_kept["dve"], 1)

            turned = kv[:, :, :].rearrange("p j d -> p (j d)").rearrange("p (b j i) -> p b j i", j=J, i=Q)

            def scan_chunk(u, j):
                n = u * J + j
                if j == 0:
                    dve.wait_ge(squared, u + 1)
                if j:
                    dve.wait_ge(gate_turned, n)
                else:
                    wait(dve, xn_turned, u * J)
                nc.vector.transpose(kvT[:, :, :].rearrange("p b i -> p (b i)"), kv[:, j, :]).then_inc(kv_turned, 1)
                dve.wait_ge(kv_turned, n + 1)
                dve.wait_ge(carry_saved, n + 1)
                nc.vector.scalar_tensor_tensor(out=kvT[:, :, 0], in0=carry[:, :], scalar=DECAY, in1=kvT[:, :, 0],
                                               op0=ALU.mult, op1=ALU.add).then_inc(carry_added, 1)
                dve.wait_ge(carry_added, n + 1)
                flat = kvT[:, :, :].rearrange("p b i -> p (b i)")
                nc.vector.tensor_tensor_scan(out=flat, data0=decay[:, :], data1=flat, initial=0.0,
                                             op0=ALU.mult, op1=ALU.add).then_inc(scanned, 1)
                dve.wait_ge(scanned, n + 1)
                if j < J - 1:
                    nc.vector.tensor_copy(carry[:, :], kvT[:, :, Q - 1]).then_inc(carry_saved, 1)
                else:
                    nc.vector.tensor_scalar(carry[:, :].bitcast(i32), kvT[:, :, Q - 1].bitcast(i32),
                                            keep[:, bass.ds(u, 1)], None, ALU.bitwise_and).then_inc(carry_saved, 1)
                nc.vector.transpose(kv[:, j, :], flat).then_inc(gate_turned, 1)

            def stats1(u, x):
                dve.wait_ge(x_loaded, (u + 1) * (G * NX))
                for j in range(J):
                    nc.vector.bn_stats(st1[:, j, :], x[:, j, :]).then_inc(stats1_done, 1)
                dve.wait_ge(stats1_done, u * J + J)
                nc.vector.memset(wait_pad[:, J:J + 1], 0.0)
                for j in range(J):
                    nc.vector.bn_aggr(mv1[:, j, :], st1[:, j, :]).then_inc(mean1_ready, 1)

            def gate(u, x, j):
                n = u * J + j
                if j == 0:
                    dve.wait_ge(rstd1_ready, u + 1)
                    dve.wait_ge(gate_turned, u * J + J)
                    dve.wait_ge(mean1_ready, u * J + J)
                nc.vector.scalar_tensor_tensor(out=kv[:, j, :], in0=x[:, j, :], scalar=mv1[:, j, 0:1], in1=kv[:, j, :],
                                               op0=ALU.subtract, op1=ALU.mult).then_inc(gated, 1)
                dve.wait_ge(gated, n + 1)
                nc.vector.scalar_tensor_tensor(out=x[:, j, :], in0=kv[:, j, :], scalar=rstd1[:, j:j + 1],
                                               in1=x[:, j, :], op0=ALU.mult, op1=ALU.add).then_inc(x1_ready, 1)
                dve.wait_ge(x1_ready, n + 1)
                nc.vector.bn_stats(st2[:, j, :], x[:, j, :]).then_inc(stats2_done, 1)
                dve.wait_ge(stats2_done, n + 1)
                nc.vector.memset(wait_pad[:, j:j + 1], 0.0)
                nc.vector.bn_aggr(mv2[:, j, :], st2[:, j, :]).then_inc(mean2_ready, 1)

            def normalise(u, x, j):
                n = u * J + j
                dve.wait_ge(rstd2_ready, n + 1)
                dve.wait_ge(mean2_ready, n + 1)
                xn = kvT[:, :, :].rearrange("p b i -> p (b i)")
                if j:
                    dve.wait_ge(xn_turned, n)
                else:
                    dve.wait_ge(gate_turned, u * J + J)
                nc.vector.tensor_scalar(xn, x[:, j, :], mv2[:, j, 0:1], rstd2[:, j:j + 1],
                                        ALU.subtract, ALU.mult).then_inc(xn_ready, 1)
                if j == 0:
                    dve.wait_ge(x1_ready, u * J + J)
                dve.wait_ge(xn_ready, n + 1)
                nc.vector.transpose(turned[:, :, j, :], xn).then_inc(xn_turned, 1)
                nc.vector.tensor_tensor(out=x[:, j, :], in0=x[:, j, :], in1=bias_row[:, :], op=ALU.add)\
                    .then_inc(bias_added, 1)

            def keep_xT_lo(u, par, c):
                dve.wait_ge(xThi_ready, u * KD + c + 1)
                hi, lo, whole = xT_slots(u, par)
                nc.vector.tensor_tensor(out=lo[:, c, :], in0=whole[:, c, :].bitcast(f32),
                                        in1=hi[:, c, :].bitcast(f32), op=ALU.subtract).then_inc(xTlo_ready, 1)

            for k in range(KH // 4):
                fold_step("WT", k)
            coefs_lo(0)
            low_products(0)
            coefs_lo(1)
            high_products(0)
            dve.wait_ge(path_product, LOWS)
            dve.wait_ge(top_loaded[0], NX)
            top_stage(nc.vector, 0).then_inc(low_matrix_ready, 1)
            low_products(1)
            high_products(1)
            dve.wait_ge(const_ready, 2)
            dve.wait_ge(bias_loaded, 4 * NX)
            nc.vector.tensor_tensor(out=bias_row[:, :], in0=bias_row[:, :], in1=bias_tmp, op=ALU.add)\
                .then_inc(bias_row_ready, 1)
            dve.wait_ge(bias_row_ready, 1)
            for j in range(J):
                scan_chunk(0, j)
            stats1(0, xs[0])
            for kind in ("regroup", "high_up", "turn_high", "high_dn", "turn_low", "back", "low_dn"):
                for i in range(sum(a == kind for a, _, _ in FOLD)):
                    fold_step(kind, i)
                    if kind == "low_dn" and i % 4 == 1:
                        keep_xT_lo(0, 0, i // 4)
                if kind == "high_up":
                    for j in range(J):
                        gate(0, xs[0], j)
                    for j in range(J):
                        normalise(0, xs[0], j)

            def finish(t, par, j):
                nc.vector.tensor_tensor(out=xs[par][:, j, :], in0=ps_y[j][:, :], in1=xs[par][:, j, :], op=ALU.add)\
                    .then_inc(out_ready, 1)

            def finish_step(t, par):
                dve.wait_ge(y_part, (t + 1) * KH)
                dve.wait_ge(bias_added, (t + 1) * J)
                for j in range(J):
                    finish(t, par, j)

            def body(t, par, first, last):
                nxt = xs[1 - par]
                for k in range(KH):
                    s = t * KH + k
                    slot = k % 2
                    dve.wait_ge(gelu_ready, s + 1)
                    wait(dve, y_part, s - 1)
                    nc.vector.tensor_copy(ghi[:, slot, :], g32[:, slot, :]).then_inc(ghi_ready, 1)
                    dve.wait_ge(ghi_ready, s + 1)
                    nc.vector.tensor_tensor(out=glo[:, slot, :], in0=g32[:, slot, :],
                                            in1=ghi[:, slot, :].bitcast(f32), op=ALU.subtract).then_inc(glo_ready, 1)
                    if k == LAG - 1 and not first:
                        finish_step(t - 1, 1 - par)
                    if last:
                        continue
                    u = t + 1
                    if 2 <= k < 2 + J:
                        scan_chunk(u, k - 2)
                    if k == 5:
                        stats1(u, nxt)
                    if 6 <= k < 8:
                        for j in range(J // 2):
                            gate(u, nxt, (k - 6) * 2 + j)
                    if 8 <= k < 10:
                        for j in range(J // 2):
                            normalise(u, nxt, (k - 8) * 2 + j)
                    if k in KEEP_AT:
                        for c in range(KD // 2):
                            keep_xT_lo(u, 1 - par, (k - KEEP_AT[0]) * 2 + c)

            steps(dve, body)
            dve.wait_ge(bias_added, T * J)
            for j in range(J):
                dve.wait_ge(y_last, j + 1)
                finish(T - 1, (T - 1) % 2, j)

        @block.tensor
        def _(pe):
            pe.wait_ge(ident_ready, 1)

            def spread(dn):
                def stage_spread(parts, rows_of, place, stage, order):
                    rows, off, n_src = src_place(stage)
                    bank, col = place
                    n = KH << (stage + 1)
                    kb = max(1, n // 512)
                    kn = KH // kb
                    for c in range(kb):
                        for i, src in enumerate(parts):
                            v = src[0:rows, off:off + n_src].rearrange(order, o=KH, a=2, b=2)
                            for bit in range(2):
                                last = nc.tensor.matmul(ps[bank + c][:, col:col + n // kb], rows_of[0:rows, bit, :],
                                                        v[:, c * kn:(c + 1) * kn, :, :, bit],
                                                        start=(i == 0 and bit == 0),
                                                        stop=(i == len(parts) - 1 and bit == 1))
                    last.then_inc(coef_spread, 1)

                def low():
                    pe.wait_ge(low_loaded[dn], LOWS * NX)
                    for stage in range(LOWS):
                        if dn:
                            pe.wait_ge(path_product, max(stage, 3) + 1)
                        if stage in PARTED:
                            i = stage - PARTED[0]
                            pe.wait_ge(sel_rounded, dn + 1)
                            pe.wait_ge(coef_lo, dn * len(PARTED) + i + 1)
                            parts, rows_of = (low_src_hi[dn], low_src_lo[dn]), sel_r[dn][:, i]
                        else:
                            if not dn:
                                pe.wait_ge(sel_ready, 2 * (stage + 1))
                            parts, rows_of = (low_src[dn],), sel[:, stage]
                        stage_spread(parts, rows_of, LOW_PLACE[stage], stage, "q (o l a b) -> q o a l b")

                def high():
                    pe.wait_ge(high_loaded[dn], HIGH_LOADS * NX)
                    if dn:
                        pe.wait_ge(path_product, UP_DONE)
                    for b in range(HIGH):
                        stage_spread((high_src[dn],), sel[:, b], HIGH_PLACE[b], b, "q (l o a b) -> q o a l b")

                return low, high

            def fold_step(kind, i):
                n = fold_at(kind, i)
                bank = ps_f[n % 3]
                if n >= 3:
                    who, count = kept_count[n - 3]
                    pe.wait_ge(fold_kept[who], count)
                if kind == "low_dn":
                    wait_kept(pe, "back", i)
                    nc.tensor.matmul(bank[:, :], LX[:, 1, i, :], wcon[:, i, :], start=True, stop=True)\
                        .then_inc(fold_made, 1)
                    return
                for c in range(4):
                    o = bank[:, c * P:(c + 1) * P]
                    block_c = slice(c * P, (c + 1) * P)
                    if kind == "WT":
                        last = nc.tensor.transpose(o, wexp[:, c, i * P:(i + 1) * P], ident[:, :])
                    elif kind == "low_up":
                        last = nc.tensor.matmul(o, WT[:, i, block_c], LX[:, 0, i, :], start=True, stop=True)
                    elif kind == "regroup":
                        last = nc.tensor.transpose(o, wexp[:, c, i * P:(i + 1) * P], ident[:, :])
                    elif kind == "high_up":
                        last = nc.tensor.matmul(o, Z[:, i, block_c], HX[:, 0, i, :], start=True, stop=True)
                    elif kind == "turn_high":
                        last = nc.tensor.transpose(o, HX[:, 1, 4 * i + c, :], ident[:, :])
                    elif kind == "high_dn":
                        last = nc.tensor.matmul(o, wcon[:, i, block_c], HX[:, 1, i, :], start=True, stop=True)
                    elif kind == "turn_low":
                        last = nc.tensor.transpose(o, LX[:, 1, 4 * i + c, :], ident[:, :])
                    elif kind == "back":
                        last = nc.tensor.transpose(o, Zd[:, c, i * P:(i + 1) * P], ident[:, :])
                last.then_inc(fold_made, 1)

            spread_low, spread_high = spread(0)
            for k in range(KH):
                if k == KH // 4:
                    spread_low()
                if k % 4 == 0:
                    pe.wait_ge(wexp_loaded[k // 4], NX)
                fold_step("WT", k)
            spread_high()
            spread_low, spread_high = spread(1)
            spread_low()
            spread_high()
            pe.wait_ge(low_matrix_ready, 1)
            for k in range(KH):
                wait_kept(pe, "WT", k)
                fold_step("low_up", k)
            wait_kept(pe, "low_up", KH - 1)
            for r in range(R):
                fold_step("regroup", r)
            pe.wait_ge(high_matrix_ready, 1)
            for r in range(R):
                wait_kept(pe, "regroup", r)
                fold_step("high_up", r)
            pe.wait_ge(path_product, spreads(1, LOW - 2))
            pe.wait_ge(bias_loaded, 4 * NX)
            nc.tensor.transpose(ps[3][:, 256:256 + 2 * KH], bias_rows, ident[0:2 * KH, 0:2 * KH]).then_inc(bcol_turned, 1)
            pe.wait_ge(high_matrix_ready, 2)
            for q in range(R // 4):
                fold_step("turn_high", q)
            pe.wait_ge(bcol_kept, 1)
            for k in range(KH):
                last = nc.tensor.matmul(ps[3][:, 256 + k:257 + k], LX[:, 0, k, :], bcol[:, k:k + 1], start=True, stop=True)
            last.then_inc(bias_low, 1)
            for r in range(R):
                if r % (R // 2) == 0:
                    pe.wait_ge(wcon_loaded[r // (R // 2)], E * NX)
                wait_kept(pe, "turn_high", r // 4)
                fold_step("high_dn", r)
            pe.wait_ge(low_matrix_ready, 2)
            for q in range(KH // 4):
                fold_step("turn_low", q)
            wait_kept(pe, "high_dn", R - 2)
            wait_kept(pe, "high_dn", R - 1)
            pe.wait_ge(yb_kept, 1)
            for k in range(KH):
                fold_step("back", k)
            wait_kept(pe, "turn_low", KH // 4 - 2)
            wait_kept(pe, "turn_low", KH // 4 - 1)
            for k in range(KH):
                fold_step("low_dn", k)

            def up_product(t, par, k):
                if k == 0:
                    pe.wait_ge(xTlo_ready, (t + 1) * KD)
                wait(pe, gelu_ready, t * KH + (k - 1))
                hi, lo, _ = xT_slots(t, par)
                terms = [(w, v) for c in range(KD) for w, v in
                         ((W1hi[:, k, c, :], hi[:, c, :]), (W1hi[:, k, c, :], lo[:, c, :]),
                          (W1lo[:, k, c, :], hi[:, c, :]))]
                for i, (w, v) in enumerate(terms):
                    last = nc.tensor.matmul(ps_h[k % 2][:, :], w, v, start=(i == 0), stop=(i == len(terms) - 1))
                last.then_inc(h_ready, 1)

            def down_product(t, k, first, ends=False):
                s = t * KH + k
                pe.wait_ge(glo_ready, s + 1)
                for j in range(J):
                    if k == 0 and not first:
                        pe.wait_ge(out_ready, (t - 1) * J + (j + 1))
                    tok = slice(j * P, (j + 1) * P)
                    for i, (g, w) in enumerate(((ghi, W2hi), (ghi, W2lo), (glo, W2hi))):
                        last = nc.tensor.matmul(ps_y[j][:, :], g[:, k % 2, tok], w[:, k, :],
                                                start=(k == 0 and i == 0), stop=(k == KH - 1 and i == 2))
                    if ends:
                        last.then_inc(y_last, 1)
                if not ends:
                    last.then_inc(y_part, 1)

            def body(t, par, first, last):
                for k in range(KH):
                    up_product(t, par, k)
                    if k >= LAG:
                        down_product(t, k - LAG, first)
                    elif not first:
                        down_product(t - 1, k - LAG + KH, False)

            steps(pe, body)
            for k in range(KH - LAG, KH):
                down_product(T - 1, k, False, ends=(k == KH - 1))


_INS = ['x', 'ctx_1024', 'L0_ffn_W_exp', 'L0_ffn_b_exp', 'L0_ffn_up_weights', 'L0_ffn_up_bias',
        'L0_ffn_down_weights', 'L0_ffn_W_con', 'L0_ffn_b_con', 'L0_ffn_down_bias']


def kernel(**inputs):
    import numpy as _np
    import concourse.bacc as _bacc
    from concourse import mybir as _mybir
    from concourse.bass_utils import run_bass_kernel_spmd as _run

    nc = _bacc.Bacc("TRN2", target_bir_lowering=False, num_devices=1)
    arrays, args = {}, []
    for name in _INS:
        a = _np.ascontiguousarray(inputs[name])
        arrays[f"in_{name}_dram"] = a
        args.append(nc.dram_tensor(f"in_{name}_dram", a.shape, _mybir.dt.from_np(a.dtype), kind="ExternalInput").ap())
    shape = inputs['x'].shape
    args.append(nc.dram_tensor("out_dram", shape, _mybir.dt.float32, kind="ExternalOutput").ap())
    xattn_ffn_program(nc, *args)
    r = _run(nc, [arrays], core_ids=[0])
    return r.results[0]["out_dram"]
```
